# Optimizing a Trainium2 kernel written in Bass

```python
import numpy as np
import jax
import jax.numpy as jnp

def _softmax(x, axis=-1):
    return jax.nn.softmax(x, axis=axis)

def _gelu(x):
    return jax.nn.gelu(x, approximate=True)

def _silu(x):
    return jax.nn.silu(x)

def _sigmoid(x):
    return jax.nn.sigmoid(x)

def _layernorm(x, axis=-1, eps=1e-05):
    m = jnp.mean(x, axis=axis, keepdims=True)
    v = jnp.var(x, axis=axis, keepdims=True)
    return (x - m) / jnp.sqrt(v + eps)

def _scatter_add(tgt, idx, src, axis=0):
    return tgt.at[idx].add(src)

def _segment_sum(src, seg, n):
    return jax.ops.segment_sum(src, seg, n)
kernel_name = 'mk_seq_preln_d1_jaxref_r8_923712'

def setup_inputs(seed: int=0):
    np.random.seed(seed)
    _w = jnp.asarray

    def _L0_attn_setup():
        import jax, jax.numpy as jnp
        import numpy as np
        D_MODEL = 128
        D_STATE = 16
        D_CONV = 4
        EXPAND = 2
        D_INNER = EXPAND * D_MODEL
        DT_RANK = (D_MODEL + 15) // 16
        BATCH = 2
        SEQLEN = 256
        key = jax.random.key(seed)
        ks = jax.random.split(key, 8)
        s = lambda k, shape, scale: jax.random.normal(k, shape, dtype=jnp.float32) * scale
        return {'x': s(ks[0], (BATCH, SEQLEN, D_MODEL), 1.0), 'W_in': s(ks[1], (D_MODEL, 2 * D_INNER), D_MODEL ** (-0.5)), 'conv_w': s(ks[2], (D_INNER, 1, D_CONV), 0.3), 'conv_b': jnp.zeros((D_INNER,), dtype=jnp.float32), 'W_x': s(ks[3], (D_INNER, DT_RANK + 2 * D_STATE), D_INNER ** (-0.5)), 'W_dt': s(ks[4], (DT_RANK, D_INNER), 2.0 * DT_RANK ** (-0.5)), 'b_dt': s(ks[5], (D_INNER,), 0.1), 'A_log': jnp.log(jnp.tile(jnp.arange(1, D_STATE + 1, dtype=jnp.float32), (D_INNER, 1))), 'D': jnp.ones((D_INNER,), dtype=jnp.float32), 'W_out': s(ks[6], (D_INNER, D_MODEL), D_INNER ** (-0.5))}
    _L0_attn_in = _L0_attn_setup()

    def _L0_ffn_setup():
        import jax, jax.numpy as jnp
        import numpy as np
        B, T, C = (4, 256, 128)
        E, FF, TOPK = (8, 256, 2)
        key = jax.random.key(seed)
        k1, k2, k3, k4 = jax.random.split(key, 4)
        s_in = 1.0 / np.sqrt(C)
        s_ff = 1.0 / np.sqrt(FF)
        return {'x': jax.random.normal(k1, (B, T, C), dtype=jnp.float32), 'gate_w': jax.random.normal(k2, (E, C), dtype=jnp.float32) * s_in, 'w1': jax.random.normal(k3, (E, FF, C), dtype=jnp.float32) * s_in, 'w2': jax.random.normal(k4, (E, C, FF), dtype=jnp.float32) * s_ff}
    _L0_ffn_in = _L0_ffn_setup()
    _d = {'L0_attn_x': _L0_attn_in['x'], 'L0_attn_W_in': _L0_attn_in['W_in'], 'L0_attn_conv_w': _L0_attn_in['conv_w'], 'L0_attn_conv_b': _L0_attn_in['conv_b'], 'L0_attn_W_x': _L0_attn_in['W_x'], 'L0_attn_W_dt': _L0_attn_in['W_dt'], 'L0_attn_b_dt': _L0_attn_in['b_dt'], 'L0_attn_A_log': _L0_attn_in['A_log'], 'L0_attn_D': _L0_attn_in['D'], 'L0_attn_W_out': _L0_attn_in['W_out'], 'L0_ffn_gate_w': _L0_ffn_in['gate_w'], 'L0_ffn_w1': _L0_ffn_in['w1'], 'L0_ffn_w2': _L0_ffn_in['w2']}
    _x0 = _d['L0_attn_x']
    _d['L0_attn_x'] = jax.random.normal(jax.random.fold_in(jax.random.key(seed), 1), (32, 256, 128), dtype=_x0.dtype)
    del _x0
    return _d

def reference(L0_attn_x, L0_attn_W_in, L0_attn_conv_w, L0_attn_conv_b, L0_attn_W_x, L0_attn_W_dt, L0_attn_b_dt, L0_attn_A_log, L0_attn_D, L0_attn_W_out, L0_ffn_gate_w, L0_ffn_w1, L0_ffn_w2):

    def _L0_attn_ref(x, W_in, conv_w, conv_b, W_x, W_dt, b_dt, A_log, D, W_out):
        import jax, jax.numpy as jnp
        import numpy as np
        D_MODEL = 128
        D_STATE = 16
        D_CONV = 4
        EXPAND = 2
        D_INNER = EXPAND * D_MODEL
        DT_RANK = (D_MODEL + 15) // 16
        BATCH = 2
        SEQLEN = 256
        dt_rank = W_dt.shape[0]
        d_state = A_log.shape[1]
        Bsz, L, _ = x.shape
        d_inner = conv_w.shape[0]
        xr = x @ W_in
        xi, res = jnp.split(xr, 2, axis=-1)
        xc = jax.lax.conv_general_dilated(xi.transpose(0, 2, 1), conv_w, window_strides=(1,), padding=[(conv_w.shape[-1] - 1, 0)], feature_group_count=d_inner) + conv_b[None, :, None]
        u = jax.nn.silu(xc.transpose(0, 2, 1))
        dbc = u @ W_x
        delta_r = dbc[..., :dt_rank]
        Bm = dbc[..., dt_rank:dt_rank + d_state]
        Cm = dbc[..., dt_rank + d_state:]
        delta = jax.nn.softplus(delta_r @ W_dt + b_dt)
        A = -jnp.exp(A_log)
        deltaA = jnp.exp(delta[..., None] * A)
        dBu = delta[..., None] * Bm[:, :, None, :] * u[..., None]

        def step(h, inp):
            dA_t, dBu_t, C_t = inp
            h = dA_t * h + dBu_t
            y_t = jnp.einsum('bdn,bn->bd', h, C_t)
            return (h, y_t)
        h0 = jnp.zeros((Bsz, d_inner, d_state), dtype=x.dtype)
        _, ys = jax.lax.scan(step, h0, (deltaA.transpose(1, 0, 2, 3), dBu.transpose(1, 0, 2, 3), Cm.transpose(1, 0, 2)))
        y = ys.transpose(1, 0, 2) + u * D
        y = y * jax.nn.silu(res)
        return y @ W_out

    def _L0_ffn_ref(x, gate_w, w1, w2):
        import jax, jax.numpy as jnp
        import numpy as np
        B, T, C = (4, 256, 128)
        E, FF, TOPK = (8, 256, 2)
        Bq, Tq, Cq = x.shape
        x_flat = x.reshape(-1, Cq)
        N = x_flat.shape[0]
        scores = x_flat @ gate_w.T
        topk_scores, topk_idx = jax.lax.top_k(scores, TOPK)
        topk_probs = jax.nn.softmax(topk_scores, axis=-1)
        cw = jnp.zeros((N, E), dtype=x_flat.dtype).at[jnp.arange(N)[:, None], topk_idx].add(topk_probs)
        y = jnp.zeros_like(x_flat)
        for e in range(E):
            h = jax.nn.silu(x_flat @ w1[e].T) @ w2[e].T
            y = y + cw[:, e:e + 1] * h
        return y.reshape(Bq, Tq, Cq)
    x = L0_attn_x
    x = x + _L0_attn_ref(_layernorm(x, axis=-1), L0_attn_W_in, L0_attn_conv_w, L0_attn_conv_b, L0_attn_W_x, L0_attn_W_dt, L0_attn_b_dt, L0_attn_A_log, L0_attn_D, L0_attn_W_out)
    x = x + _L0_ffn_ref(_layernorm(x, axis=-1), L0_ffn_gate_w, L0_ffn_w1, L0_ffn_w2)
    return x

_drawn_inputs = setup_inputs


def setup_inputs(seed=0):
    import zlib

    import numpy as np

    out = dict(_drawn_inputs(seed))
    spreads = {'L0_attn_conv_b': (0.0, 0.1), 'L0_attn_D': (1.0, 0.2)}
    factors = {'L0_attn_b_dt': 3.332}
    for name, (base, spread) in spreads.items():
        noise = np.random.default_rng([zlib.crc32(name.encode()), seed]).standard_normal(out[name].shape)
        drawn = base * np.exp(spread * noise) if base else spread * noise
        out[name] = jnp.asarray(drawn.astype(out[name].dtype))
    for name, factor in factors.items():
        out[name] = (out[name] * factor).astype(out[name].dtype)
    return out
```

```python
from contextlib import ExitStack

import concourse.bass as bass
from concourse import mybir

ALU = mybir.AluOpType
ACT = mybir.ActivationFunctionType
F32 = mybir.dt.float32
BF16 = mybir.dt.bfloat16
U32 = mybir.dt.uint32

P = 128
SEQ = 256
SEQS = 2
T = SEQS * SEQ
TB = T // P
C = 128
H = 2
NS = 16
GROUP = 4
NG = NS // GROUP
CH = H * NG
PAIR = 2
PU = 2 * GROUP // PAIR
RANK = 8
TAPS = 4
E = 8
FH = 2
SPLIT = 32
EPS = 1e-5


class Round:

    def __init__(self, at, loop=None):
        self.at, self.loop = at, loop
        self.odd = at % 2

    def later(self, k):
        return Round(self.at + k, self.loop)

    def count(self, per, more):
        v = self.at * per + more
        return v if self.loop is None else self.loop * (2 * per) + v

    def turn(self, per, more):
        v = self.at // 2 * per + more
        return v if self.loop is None else self.loop * per + v

    def number(self):
        return self.at if self.loop is None else self.loop * 2 + self.at


def mamba_moe(nc, x, W_in, conv_w, conv_b, W_x, W_dt, b_dt, A_log, D, W_out, gate_wT, w1T, w2T, out):
    rounds = x.shape[0] * x.shape[1] // T
    x_v = x.rearrange("(i s) (b p) c -> i p (s b) c", s=SEQS, p=P)
    out_v = out.rearrange("(i s) (b p) c -> i p (s b) c", s=SEQS, p=P)

    def there(*js):
        return all(j.loop is not None or 0 <= j.at < rounds for j in js)

    def wait(eng, sem, value):
        if not isinstance(value, int) or value > 0:
            eng.wait_ge(sem, value)

    def run(eng, body, first, last, loop_first, loop_last):
        for i in range(first, loop_first):
            body(Round(i))
        pairs = (loop_last - loop_first + 1) // 2
        with eng.Fori(0, pairs) as it:
            body(Round(loop_first, it))
            body(Round(loop_first + 1, it))
        for i in range(loop_first + 2 * pairs, last + 1):
            body(Round(i))

    with ExitStack() as ctx:
        def sb(name, shape, dt=F32):
            return ctx.enter_context(nc.sbuf_tensor(name, shape, dt))

        def ps(name, shape):
            return ctx.enter_context(nc.psum_tensor(name, shape, F32))

        def sem(name):
            return ctx.enter_context(nc.semaphore(name))

        w_in = sb("w_in", [P, 4 * P])
        w_bc = sb("w_bc", [P, H, P])
        w_dt = sb("w_dt", [P, H * P])
        w_out = sb("w_out", [P, H, C])
        taps_w = sb("taps_w", [P, H, TAPS])
        conv_bias = sb("conv_bias", [P, H])
        dt_bias = sb("dt_bias", [P, H])
        skip_w = sb("skip_w", [P, H])
        a_neg = sb("a_neg", [P, H, NS])
        gate_w = sb("gate_w", [C, E])
        w1 = sb("w1", [C, E, FH, P])
        w2 = sb("w2", [P, FH, E, C])
        ident = sb("ident", [P, P])
        select = sb("select", [3 * SPLIT, 2 * NS, P], BF16)
        expert_no = sb("expert_no", [P, E])
        power = sb("power", [P, TB])
        x_in = sb("x_in", [P, 2, TB, C])
        stats = sb("stats", [P, 2, TB, 6])
        moments = sb("moments", [P, 2, 3, TB])
        mean = sb("mean", [P, 2, TB])
        variance = sb("variance", [P, 2, TB])
        rstd = sb("rstd", [P, 2, TB])
        xn = sb("xn", [P, 2, TB, C])
        xnT = sb("xnT", [C, T])
        tap = sb("tap", [P, H, TAPS - 1, SEQS, TAPS - 1 + SEQ])
        u = sb("u", [P, 2, H, T])
        gate = sb("gate", [P, 2, H, T])
        bcd = sb("bcd", [P, T])
        rest = sb("rest", [3 * SPLIT, T])
        mid = sb("mid", [3 * SPLIT, T], BF16)
        parts = sb("parts", [3 * SPLIT, 2, T], BF16)
        soft = sb("soft", [P, H, T])
        delta = sb("delta", [P, 2, H, T])
        du = sb("du", [P, 2, H, T])
        dA = sb("dA", [P, 4, GROUP, T])
        h = sb("h", [P, 2, GROUP, T])
        yT = sb("yT", [P, TB, P])
        yg = sb("yg", [P, H, T])
        x_again = sb("x_again", [P, 2, TB, C])
        x1 = sb("x1", [P, 2, TB, C])
        x2T = sb("x2T", [C, 2, T])
        scores = sb("scores", [P, TB, E])
        top = sb("top", [P, TB, 8])
        top_at = sb("top_at", [P, TB, 8], U32)
        top_no = sb("top_no", [P, TB, 2])
        ratio = sb("ratio", [P, TB])
        prob = sb("prob", [P, 3, TB])
        picked = sb("picked", [P, 2, TB, E])
        cw = sb("cw", [P, 2, TB, E])
        hid = sb("hid", [P, 2, FH, T])

        pair_ps = ps("pair_ps", [P, 2, PAIR, T])
        y_ps = ps("y_ps", [P, TB, P])
        expert_ps = ps("expert_ps", [P, TB, C])
        bank = [ps("bank0", [P, T]), ps("bank1", [P, T])]

        weights_loaded = sem("weights_loaded")
        zeros_set = sem("zeros_set")
        constants_ready = sem("constants_ready")
        a_exp_ready = sem("a_exp_ready")
        a_ready = sem("a_ready")
        x_loaded = [sem("x_loaded0"), sem("x_loaded1")]
        x_again_loaded = [sem("x_again_loaded0"), sem("x_again_loaded1")]
        out_stored = [sem("out_stored0"), sem("out_stored1")]
        stats_ready = [sem("stats_ready0"), sem("stats_ready1")]
        moments_ready = [sem("moments_ready0"), sem("moments_ready1")]
        variance_ready = [sem("variance_ready0"), sem("variance_ready1")]
        rstd_ready = [sem("rstd_ready0"), sem("rstd_ready1")]
        xn_ready = [sem("xn_ready0"), sem("xn_ready1")]
        xn_turned = sem("xn_turned")
        xnT_ready = sem("xnT_ready")
        projected = sem("projected")
        taps_ready = sem("taps_ready")
        gate_ready = sem("gate_ready")
        conv_added = sem("conv_added")
        u_ready = sem("u_ready")
        bcd_projected = sem("bcd_projected")
        bcd_ready = sem("bcd_ready")
        high_ready = sem("high_ready")
        split_step = sem("split_step")
        dt_projected = sem("dt_projected")
        dt_read = sem("dt_read")
        soft_exp = sem("soft_exp")
        soft_ready = sem("soft_ready")
        delta_ready = sem("delta_ready")
        du_ready = sem("du_ready")
        pair_ready = sem("pair_ready")
        dA_ready = sem("dA_ready")
        pair_used = sem("pair_used")
        scan_done = sem("scan_done")
        y_added = sem("y_added")
        yT_ready = sem("yT_ready")
        y_turned = sem("y_turned")
        skip_added = sem("skip_added")
        gated = sem("gated")
        attn_projected = sem("attn_projected")
        x1_ready = sem("x1_ready")
        xn2_turned = sem("xn2_turned")
        x2T_ready = sem("x2T_ready")
        scored = sem("scored")
        scores_ready = sem("scores_ready")
        top_ready = sem("top_ready")
        top_gap = sem("top_gap")
        top_at_ready = sem("top_at_ready")
        ratio_ready = sem("ratio_ready")
        routing_step = sem("routing_step")
        hid_projected = sem("hid_projected")
        hid_ready = sem("hid_ready")
        expert_done = sem("expert_done")
        expert_added = sem("expert_added")

        LOADS = 15
        CONSTANTS = 8 + E
        block = ctx.enter_context(nc.Block())

        @block.sync
        def _(sp):
            def load(dst, src):
                sp.dma_start(dst, src).then_inc(weights_loaded, 16)

            def start_round(i):
                nxt = i.later(2)
                if there(nxt):
                    wait(sp, xn_ready[0], nxt.count(1, -1))
                    sp.dma_start(x_in[:, nxt.odd], x_v[nxt.number()]).then_inc(x_loaded[nxt.odd], 16)
                if there(i):
                    wait(sp, x1_ready, i.count(1, -1))
                    sp.dma_start(x_again[:, i.odd], x_v[i.number()]).then_inc(x_again_loaded[i.odd], 16)
                done = i.later(-3)
                if there(done):
                    wait(sp, expert_added, done.count(E, E))
                    sp.dma_start(out_v[done.number()], x1[:, done.odd]).then_inc(out_stored[done.odd], 16)

            start_round(Round(-2))
            load(w_in[:, :], W_in)
            start_round(Round(-1))
            load(taps_w[:, :, :], conv_w.rearrange("(h p) o k -> p h (o k)", p=P))
            load(conv_bias[:, :], conv_b)
            for part in range(3):
                load(w_bc[:, :, part * SPLIT:(part + 1) * SPLIT],
                     W_x[:, RANK:RANK + 2 * NS].rearrange("(h p) n -> p h n", p=P))
            load(w_bc[:, :, 3 * SPLIT:3 * SPLIT + RANK], W_x[:, 0:RANK].rearrange("(h p) n -> p h n", p=P))
            load(w_dt[3 * SPLIT:3 * SPLIT + RANK, :], W_dt)
            load(dt_bias[:, :], b_dt)
            load(a_neg[:, :, :], A_log.rearrange("(h p) n -> p h n", p=P))
            load(skip_w[:, :], D)
            load(w_out[:, :, :], W_out.rearrange("(h p) c -> p h c", p=P))
            load(w1[:, :, :, :], w1T.rearrange("c (e h f) -> c e h f", e=E, h=FH))
            load(w2[:, :, :, :], w2T.rearrange("(h p) e c -> p h e c", p=P))
            sp.dma_start(gate_w[:, :], gate_wT).then_inc(weights_loaded, 16)
            run(sp, start_round, 0, rounds + 2, 3, rounds - 3)
            for odd in range(2):
                sp.wait_ge(out_stored[odd], 16 * (rounds // 2))

        @block.gpsimd
        def _(pool):
            nc.gpsimd.memset(ident[:, :], 0.0).then_inc(zeros_set, 1)
            nc.gpsimd.memset(select[:, :, :], 0.0).then_inc(zeros_set, 1)
            nc.gpsimd.memset(tap[:, :, :, :, :], 0.0).then_inc(constants_ready, 1)
            nc.gpsimd.memset(dA[:, :, :, :], 0.0).then_inc(constants_ready, 1)
            nc.gpsimd.memset(w_bc[:, :, 3 * SPLIT + RANK:], 0.0).then_inc(constants_ready, 1)
            nc.gpsimd.memset(power[:, :], -0.5).then_inc(constants_ready, 1)
            for e in range(E):
                nc.gpsimd.memset(expert_no[:, e:e + 1], float(e)).then_inc(constants_ready, 1)
            pool.wait_ge(zeros_set, 2)
            nc.gpsimd.affine_select(out=ident[:, :], in_=ident[:, :], compare_op=ALU.not_equal, fill=1.0,
                                    base=0, pattern=[[-1, P]], channel_multiplier=1).then_inc(constants_ready, 1)
            for part in range(3):
                nc.gpsimd.affine_select(out=select[:, :, :], in_=select[:, :, :], compare_op=ALU.not_equal,
                                        fill=1.0, base=-part * SPLIT, pattern=[[-1, 2 * NS], [0, P]],
                                        channel_multiplier=1).then_inc(constants_ready, 1)
                pool.wait_ge(constants_ready, 5 + E + part + 1)

            def inverse_deviation(j, k):
                if not there(j):
                    return
                pool.wait_ge(variance_ready[k], j.count(1, 1))
                wait(pool, xn_ready[k], j.count(1, 0))
                nc.gpsimd.tensor_tensor(rstd[:, k, :], variance[:, k, :], power[:, 0:TB],
                                        ALU.pow).then_inc(rstd_ready[k], 1)

            def convolve(j):
                if not there(j):
                    return
                odd = j.odd
                for k in range(TAPS - 1):
                    for half in range(H):
                        if k == 0:
                            pool.wait_ge(taps_ready, j.count(H, half + 1))
                        else:
                            pool.wait_ge(conv_added, j.count(H * (TAPS - 1), H * (k - 1) + half + 1))
                        at = u[:, odd, half, :].rearrange("p (s t) -> p s t", s=SEQS)
                        nc.gpsimd.tensor_tensor(at, at, tap[:, half, k, :, k:k + SEQ], ALU.add).then_inc(conv_added, 1)

            def split_and_delta(j, post):
                if not there(j):
                    return
                odd = j.odd
                pool.wait_ge(conv_added, j.count(H * (TAPS - 1), H * (TAPS - 1)))
                if there(post):
                    pool.wait_ge(rstd_ready[1], post.count(1, 1))
                pool.wait_ge(high_ready, j.count(1, 1))
                second, third = slice(SPLIT, 2 * SPLIT), slice(2 * SPLIT, 3 * SPLIT)
                nc.gpsimd.tensor_tensor(rest[third, :], bcd[third, :], parts[third, odd, :], ALU.subtract)
                nc.gpsimd.tensor_tensor(mid[third, :], bcd[third, :], parts[third, odd, :],
                                        ALU.subtract).then_inc(split_step, 1)
                pool.wait_ge(split_step, j.count(3, 1))
                nc.gpsimd.tensor_tensor(parts[second, odd, :], bcd[second, :], parts[second, odd, :],
                                        ALU.subtract).then_inc(split_step, 1)
                pool.wait_ge(split_step, j.count(3, 2))
                nc.gpsimd.tensor_tensor(parts[third, odd, :], rest[third, :], mid[third, :],
                                        ALU.subtract).then_inc(split_step, 1)
                pool.wait_ge(split_step, j.count(3, 3))
                pool.wait_ge(soft_ready, j.count(1, 1))
                nc.gpsimd.tensor_tensor(delta[:, odd], delta[:, odd], soft[:, :, :], ALU.add).then_inc(delta_ready, 1)
                pool.wait_ge(delta_ready, j.count(1, 1))
                pool.wait_ge(u_ready, j.count(H, H))
                wait(pool, pair_used, j.count(CH * PU, -CH * PU))
                nc.gpsimd.tensor_tensor(du[:, odd], delta[:, odd], u[:, odd], ALU.mult).then_inc(du_ready, 1)

            def round_(i):
                pre, post = i.later(1), i.later(-1)
                inverse_deviation(pre, 0)
                convolve(pre)
                inverse_deviation(post, 1)
                split_and_delta(pre, post)

            run(pool, round_, -1, rounds, 1, rounds - 2)

        @block.scalar
        def _(act):
            act.wait_ge(weights_loaded, 16 * LOADS)
            act.wait_ge(constants_ready, CONSTANTS)
            nc.scalar.activation(a_neg[:, :, :], a_neg[:, :, :], ACT.Exp).then_inc(a_exp_ready, 1)

            def decay(j, c):
                if not there(j):
                    return
                if c == 0:
                    act.wait_ge(delta_ready, j.count(1, 1))
                wait(act, scan_done, j.count(CH, c - 3))
                half, g = divmod(c, NG)
                src = delta[:, j.odd, half, :].rearrange("p (s t) -> p s t", s=SEQS)[:, :, 1:SEQ]
                for n in range(GROUP):
                    dst = dA[:, c % 4, n, :].rearrange("p (s t) -> p s t", s=SEQS)[:, :, 1:SEQ]
                    k = g * GROUP + n
                    last = nc.scalar.activation(dst, src, ACT.Exp, scale=a_neg[:, half, k:k + 1])
                last.then_inc(dA_ready, 1)

            def copy_y(j, half):
                if not there(j):
                    return
                act.wait_ge(y_added, j.count(CH, NG * (half + 1)))
                wait(act, y_turned, j.count(H, half))
                nc.scalar.activation(yT[:, :, :], y_ps[:, :, :], ACT.Copy).then_inc(yT_ready, 1)

            def hidden(j, e):
                if not there(j):
                    return
                wait(act, expert_done, j.count(E, e - 1))
                for f in range(FH):
                    act.wait_ge(hid_projected, j.count(E * FH, FH * e + f + 1))
                    nc.scalar.activation(hid[:, e % 2, f, :], bank[f][:, :], ACT.Silu).then_inc(hid_ready, 1)

            def round_(i):
                pre, post, moe = i.later(1), i.later(-1), i.later(-2)
                decay(i, 2)
                copy_y(post, 1)
                decay(i, 3)
                if there(pre):
                    act.wait_ge(xn_turned, pre.count(1, 1))
                    wait(act, projected, pre.count(4, 0))
                    nc.scalar.activation(xnT[:, :], bank[0][:, :], ACT.Copy).then_inc(xnT_ready, 1)
                hidden(moe, 0)
                hidden(moe, 1)
                if there(pre):
                    wait(act, gated, pre.count(H, -H))
                    wait(act, conv_added, pre.count(H * (TAPS - 1), 0))
                    for half in range(H):
                        act.wait_ge(projected, pre.count(4, half + 1))
                        for k in range(TAPS - 1):
                            nc.scalar.activation(tap[:, half, k, :, TAPS - 1:],
                                                 bank[half][:, :].rearrange("p (s t) -> p s t", s=SEQS),
                                                 ACT.Copy, scale=taps_w[:, half, k:k + 1])
                        nc.scalar.activation(u[:, pre.odd, half, :], bank[half][:, :], ACT.Identity,
                                             scale=taps_w[:, half, TAPS - 1:TAPS],
                                             bias=conv_bias[:, half:half + 1]).then_inc(taps_ready, 1)
                    for half in range(H):
                        act.wait_ge(projected, pre.count(4, 2 + half + 1))
                        nc.scalar.activation(gate[:, pre.odd, half, :], bank[half][:, :],
                                             ACT.Silu).then_inc(gate_ready, 1)
                decay(i, 4)
                decay(i, 5)
                if there(pre):
                    for half in range(H):
                        act.wait_ge(conv_added, pre.count(H * (TAPS - 1), H * (TAPS - 2) + half + 1))
                        nc.scalar.activation(u[:, pre.odd, half, :], u[:, pre.odd, half, :],
                                             ACT.Silu).then_inc(u_ready, 1)
                hidden(moe, 2)
                hidden(moe, 3)
                if there(pre):
                    act.wait_ge(bcd_projected, pre.count(1, 1))
                    wait(act, split_step, pre.count(3, 0))
                    wait(act, dt_projected, pre.count(H, 0))
                    nc.scalar.activation(bcd[0:3 * SPLIT + RANK, :], bank[0][0:3 * SPLIT + RANK, :],
                                         ACT.Copy).then_inc(bcd_ready, 1)
                    wait(act, pair_ready, pre.count(CH * PU, -CH * PU))
                    nc.scalar.activation(parts[:, pre.odd, :], bank[0][0:3 * SPLIT, :],
                                         ACT.Copy).then_inc(high_ready, 1)
                decay(i, 6)
                copy_y(i, 0)
                if there(post):
                    act.wait_ge(xn2_turned, post.count(1, 1))
                    wait(act, hid_projected, post.count(E * FH, -E * FH))
                    nc.scalar.activation(x2T[:, post.odd, :], bank[1][:, :], ACT.Copy).then_inc(x2T_ready, 1)
                decay(i, 7)
                if there(pre):
                    wait(act, du_ready, pre.count(1, -1))
                    for half in range(H):
                        act.wait_ge(dt_projected, pre.count(H, half + 1))
                        nc.scalar.activation(soft[:, half, :], bank[half][:, :], ACT.Abs,
                                             bias=dt_bias[:, half:half + 1])
                        nc.scalar.activation(delta[:, pre.odd, half, :], bank[half][:, :], ACT.Relu,
                                             bias=dt_bias[:, half:half + 1]).then_inc(dt_read, 1)
                    act.wait_ge(dt_read, pre.count(H, H))
                    nc.scalar.activation(soft[:, :, :], soft[:, :, :], ACT.Exp, scale=-1.0).then_inc(soft_exp, 1)
                    act.wait_ge(soft_exp, pre.count(1, 1))
                    nc.scalar.activation(soft[:, :, :], soft[:, :, :], ACT.Ln, bias=1.0).then_inc(soft_ready, 1)
                hidden(moe, 4)
                hidden(moe, 5)
                if there(post):
                    act.wait_ge(top_gap, post.count(1, 1))
                    nc.scalar.activation(ratio[:, :], ratio[:, :], ACT.Exp).then_inc(ratio_ready, 1)
                decay(pre, 0)
                decay(pre, 1)
                hidden(moe, 6)
                hidden(moe, 7)

            act.wait_ge(a_ready, 1)
            run(act, round_, -1, rounds + 1, 3, rounds - 2)

        @block.vector
        def _(dve):
            def over_pair(ap):
                return ap.unsqueeze(1).broadcast_to([P, PAIR, T])

            def inputs(j, c, p):
                half = c // NG
                if p == 0:
                    if c == 0:
                        dve.wait_ge(du_ready, j.count(1, 1))
                    wait(dve, y_added, j.count(CH, c - 1))
                dve.wait_ge(pair_ready, j.count(CH * PU, c * PU + p + 1))
                nc.vector.tensor_tensor(h[:, c % 2, PAIR * p:PAIR * p + PAIR, :], over_pair(du[:, j.odd, half, :]),
                                        pair_ps[:, p % 2], ALU.mult).then_inc(pair_used, 1)

            def scan(j, c):
                dve.wait_ge(pair_used, j.count(CH * PU, c * PU + PU // 2))
                dve.wait_ge(dA_ready, j.count(CH, c + 1))
                run_ = h[:, c % 2].rearrange("p n t -> p (n t)")
                nc.vector.tensor_tensor_scan(run_, dA[:, c % 4].rearrange("p n t -> p (n t)"), run_, 0.0,
                                             ALU.mult, ALU.add).then_inc(scan_done, 1)

            def outputs(j, c, p):
                dve.wait_ge(pair_ready, j.count(CH * PU, c * PU + PU // 2 + p + 1))
                dve.wait_ge(scan_done, j.count(CH, c + 1))
                at = h[:, c % 2, PAIR * p:PAIR * p + PAIR, :]
                nc.vector.tensor_tensor(at, at, pair_ps[:, p % 2], ALU.mult).then_inc(pair_used, 1)

            def norm_stats(j, k, src):
                for b in range(TB):
                    last = nc.vector.bn_stats(stats[:, k, b, :], src[:, b, :])
                last.then_inc(stats_ready[k], 1)
                even, odd = ([stats[:, k, :, 3 * o + v] for v in (1, 2)] for o in range(2))
                total, gap, spread = (moments[:, k, v, :] for v in range(3))
                dve.wait_ge(stats_ready[k], j.count(1, 1))
                nc.vector.tensor_tensor(total, even[0], odd[0], ALU.add)
                nc.vector.tensor_tensor(gap, even[0], odd[0], ALU.subtract)
                nc.vector.tensor_tensor(spread, even[1], odd[1], ALU.add).then_inc(moments_ready[k], 1)
                dve.wait_ge(moments_ready[k], j.count(3, 1))
                nc.vector.tensor_scalar(mean[:, k, :], total, 0.5, None, ALU.mult)
                nc.vector.scalar_tensor_tensor(out=gap, in0=gap, scalar=C / 4, in1=gap, op0=ALU.mult,
                                               op1=ALU.mult).then_inc(moments_ready[k], 1)
                dve.wait_ge(moments_ready[k], j.count(3, 2))
                nc.vector.tensor_tensor(spread, spread, gap, ALU.add).then_inc(moments_ready[k], 1)
                dve.wait_ge(moments_ready[k], j.count(3, 3))
                nc.vector.tensor_scalar(variance[:, k, :], spread, 1.0 / C, EPS, ALU.mult,
                                        ALU.add).then_inc(variance_ready[k], 1)

            def norm_apply(j, k, src, turned):
                dve.wait_ge(rstd_ready[k], j.count(1, 1))
                wait(dve, turned, j.count(1, 0))
                for b in range(TB):
                    last = nc.vector.tensor_scalar(xn[:, k, b, :], src[:, b, :], mean[:, k, b:b + 1],
                                                   rstd[:, k, b:b + 1], ALU.subtract, ALU.mult)
                last.then_inc(xn_ready[k], 1)

            def pre_norm(j):
                if there(j):
                    dve.wait_ge(x_loaded[j.odd], j.turn(16, 16))
                    norm_stats(j, 0, x_in[:, j.odd])
                    norm_apply(j, 0, x_in[:, j.odd], xn_turned)

            def gating(j, half):
                if not there(j):
                    return
                dve.wait_ge(y_turned, j.count(H, half + 1))
                wait(dve, attn_projected, j.count(1, 0))
                nc.vector.scalar_tensor_tensor(out=yg[:, half, :], in0=u[:, j.odd, half, :],
                                               scalar=skip_w[:, half:half + 1], in1=bank[half][:, :],
                                               op0=ALU.mult, op1=ALU.add).then_inc(skip_added, 1)
                dve.wait_ge(skip_added, j.count(H, half + 1))
                dve.wait_ge(gate_ready, j.count(H, H))
                nc.vector.tensor_tensor(yg[:, half, :], yg[:, half, :], gate[:, j.odd, half, :],
                                        ALU.mult).then_inc(gated, 1)

            def residual(j):
                if there(j):
                    dve.wait_ge(attn_projected, j.count(1, 1))
                    dve.wait_ge(x_again_loaded[j.odd], j.turn(16, 16))
                    wait(dve, out_stored[j.odd], j.turn(16, 0))
                    nc.vector.tensor_tensor(x1[:, j.odd], x_again[:, j.odd],
                                            bank[0][:, :].rearrange("p (b c) -> p b c", b=TB),
                                            ALU.add).then_inc(x1_ready, 1)

            def post_stats(j):
                if there(j):
                    dve.wait_ge(x1_ready, j.count(1, 1))
                    norm_stats(j, 1, x1[:, j.odd])

            def post_norm(j):
                if there(j):
                    norm_apply(j, 1, x1[:, j.odd], xn2_turned)

            def top_two(j):
                if not there(j):
                    return
                dve.wait_ge(scored, j.count(1, 1))
                in_bank = bank[1][:, 0:TB * E].rearrange("p (b e) -> p b e", b=TB)
                nc.vector.tensor_copy(scores[:, :, :], in_bank).then_inc(scores_ready, 1)
                for b in range(TB):
                    last = nc.vector.max(out=top[:, b, :], in_=in_bank[:, b, :])
                last.then_inc(top_ready, 1)
                dve.wait_ge(scores_ready, j.count(1, 1))
                dve.wait_ge(top_ready, j.count(1, 1))
                nc.vector.tensor_tensor(ratio[:, :], top[:, :, 1], top[:, :, 0], ALU.subtract).then_inc(top_gap, 1)
                for b in range(TB):
                    last = nc.vector.max_index(top_at[:, b, :], top[:, b, :], scores[:, b, :])
                last.then_inc(top_at_ready, 1)

            def routing(j):
                if not there(j):
                    return
                step = 0

                def then(ins):
                    nonlocal step
                    step += 1
                    ins.then_inc(routing_step, 1)

                def so_far():
                    dve.wait_ge(routing_step, j.count(8, step))

                dve.wait_ge(ratio_ready, j.count(1, 1))
                dve.wait_ge(top_at_ready, j.count(1, 1))
                then(nc.vector.tensor_scalar(prob[:, 0, :], ratio[:, :], 1.0, None, ALU.add))
                then(nc.vector.tensor_copy(top_no[:, :, :], top_at[:, :, 0:2]))
                so_far()
                then(nc.vector.reciprocal(prob[:, 1, :], prob[:, 0, :]))
                for k in range(2):
                    no = top_no[:, :, k:k + 1].broadcast_to([P, TB, E])
                    then(nc.vector.tensor_tensor(picked[:, k], expert_no[:, :].unsqueeze(1).broadcast_to([P, TB, E]),
                                                 no, ALU.is_equal))
                so_far()
                nc.vector.tensor_tensor(prob[:, 2, :], ratio[:, :], prob[:, 1, :], ALU.mult).then_inc(routing_step, 1)
                step += 1
                so_far()
                for k in range(2):
                    pk = prob[:, 1 + k, :].unsqueeze(2).broadcast_to([P, TB, E])
                    last = nc.vector.tensor_tensor(picked[:, k], picked[:, k], pk, ALU.mult)
                then(last)
                so_far()
                then(nc.vector.tensor_tensor(cw[:, j.odd], picked[:, 0], picked[:, 1], ALU.add))

            def add_expert(j, e):
                if not there(j):
                    return
                dve.wait_ge(expert_done, j.count(E, e + 1))
                if e == 0:
                    dve.wait_ge(routing_step, j.count(8, 8))
                else:
                    dve.wait_ge(expert_added, j.count(E, e))
                for b in range(TB):
                    last = nc.vector.scalar_tensor_tensor(out=x1[:, j.odd, b, :], in0=expert_ps[:, b, :],
                                                          scalar=cw[:, j.odd, b, e:e + 1], in1=x1[:, j.odd, b, :],
                                                          op0=ALU.mult, op1=ALU.add)
                last.then_inc(expert_added, 1)

            def round_(i):
                pre, post, moe, old = i.later(1), i.later(-1), i.later(-2), i.later(-3)
                now = there(i)
                for c in range(CH):
                    if c == 0:
                        pre_norm(pre)
                    if now:
                        inputs(i, c, 0)
                        inputs(i, c, 1)
                        scan(i, c)
                    m, e = (old, E - 2) if c == 0 else (moe, c - 2)
                    if c % 2 == 0:
                        add_expert(m, e)
                    if c == 1:
                        gating(post, 1)
                    if c == 2:
                        residual(post)
                    if c == 3:
                        post_norm(post)
                    if c == 5:
                        gating(i, 0)
                    if c == 7:
                        routing(post)
                    if now:
                        outputs(i, c, 0)
                    if c == 2:
                        post_stats(post)
                    if now:
                        outputs(i, c, 1)
                    if c % 2 == 0:
                        add_expert(m, e + 1)
                    if c == 5:
                        top_two(post)

            dve.wait_ge(constants_ready, CONSTANTS)
            dve.wait_ge(weights_loaded, 16 * LOADS)
            dve.wait_ge(a_exp_ready, 1)
            nc.vector.tensor_scalar(a_neg[:, :, :], a_neg[:, :, :], -1.0, None, ALU.mult).then_inc(a_ready, 1)
            run(dve, round_, -1, rounds + 2, 3, rounds - 2)

        @block.tensor
        def _(pe):
            def free(*uses):
                for s, j, per, more in uses:
                    if there(j):
                        pe.wait_ge(s, j.count(per, more))
                        return

            def pair(j, c, q):
                if not there(j):
                    return
                if c == 0 and q == 0:
                    pe.wait_ge(split_step, j.count(3, 3))
                wait(pe, pair_used, j.count(CH * PU, c * PU + q - 1))
                row = (NS if q >= PU // 2 else 0) + c % NG * GROUP + q % 2 * PAIR
                for n in range(PAIR):
                    last = nc.tensor.matmul(pair_ps[:, q % 2, n, :], select[:, row + n, :], parts[:, j.odd, :],
                                            start=True, stop=True)
                last.then_inc(pair_ready, 1)

            def sum_states(j, c):
                if not there(j):
                    return
                half, g = divmod(c, NG)
                pe.wait_ge(pair_used, j.count(CH * PU, c * PU + PU))
                if g == 0:
                    wait(pe, yT_ready, j.count(H, half))
                for n in range(GROUP):
                    for b in range(TB):
                        last = nc.tensor.matmul(y_ps[:, b, :], h[:, c % 2, n, b * P:(b + 1) * P], ident[:, :],
                                                is_transpose=True, start=(g == 0 and n == 0 and b == 0),
                                                stop=(g == NG - 1 and n == GROUP - 1), skip_group_check=True)
                last.then_inc(y_added, 1)

            def turn(dst, src, signal):
                for b in range(TB):
                    last = nc.tensor.transpose(dst[:, b * P:(b + 1) * P], src[:, b, :], ident[:, :])
                last.then_inc(signal, 1)

            def hidden(j, e, f, uses):
                if not there(j):
                    return
                if e == 0 and f == 0:
                    pe.wait_ge(x2T_ready, j.count(1, 1))
                free(*uses)
                nc.tensor.matmul(bank[f][:, :], w1[:, e, f, :], x2T[:, j.odd, :], start=True,
                                 stop=True).then_inc(hid_projected, 1)

            def expert(j, e):
                if not there(j):
                    return
                pe.wait_ge(hid_ready, j.count(E * FH, FH * (e + 1)))
                wait(pe, expert_added, j.count(E, e))
                for b in range(TB):
                    for f in range(FH):
                        last = nc.tensor.matmul(expert_ps[:, b, :], hid[:, e % 2, f, b * P:(b + 1) * P],
                                                w2[:, f, e, :], start=(f == 0), stop=(f == FH - 1))
                last.then_inc(expert_done, 1)

            def round_(i):
                pre, post, moe, old = i.later(1), i.later(-1), i.later(-2), i.later(-3)

                def hid_use(j, e, f):
                    return (hid_ready, j, E * FH, FH * e + f + 1)

                use_xnT = (xnT_ready, pre, 1, 1)
                use_taps = [(taps_ready, pre, H, f + 1) for f in range(H)]
                use_gate = [(gate_ready, pre, H, f + 1) for f in range(H)]
                use_attn = (x1_ready, post, 1, 1)
                use_bcd = (high_ready, pre, 1, 1)
                use_x2T = (x2T_ready, post, 1, 1)
                use_dt = [(dt_read, pre, H, f + 1) for f in range(H)]
                use_scores = (top_ready, post, 1, 1)
                use_y1 = (skip_added, post, H, 2)
                use_y0 = (skip_added, i, H, 1)
                last_scores = (top_ready, i.later(-2), 1, 1)
                last_dt = [(dt_read, i, H, f + 1) for f in range(H)]

                sum_states(post, 7)
                expert(old, E - 2)
                pair_c(i, 0)
                if there(pre):
                    pe.wait_ge(xn_ready[0], pre.count(1, 1))
                    free(hid_use(old, 7, 0), last_dt[0], (skip_added, post, H, 1))
                    turn(bank[0], xn[:, 0], xn_turned)
                if there(post):
                    pe.wait_ge(yT_ready, post.count(H, 2))
                    free(hid_use(old, 7, 1), last_scores, last_dt[1])
                    turn(bank[1], yT, y_turned)
                expert(old, E - 1)
                pair_b(i, 1)
                sum_states(i, 0)
                hidden(moe, 0, 0, [use_xnT, hid_use(old, 7, 0)])
                hidden(moe, 0, 1, [use_y1])
                pair_c(i, 1)
                hidden(moe, 1, 0, [hid_use(moe, 0, 0)])
                hidden(moe, 1, 1, [hid_use(moe, 0, 1)])
                if there(pre):
                    pe.wait_ge(xnT_ready, pre.count(1, 1))
                    for f in range(2 * H):
                        if f >= H:
                            free(use_taps[f - H])
                        else:
                            free(hid_use(moe, 1, f), *([use_xnT] if f == 0 else [use_y1, last_dt[1]]))
                        nc.tensor.matmul(bank[f % H][:, :], w_in[:, f * P:(f + 1) * P], xnT[:, :], start=True,
                                         stop=True).then_inc(projected, 1)
                pair_b(i, 2)
                sum_states(i, 1)
                expert(moe, 0)
                pair_c(i, 2)
                if there(post):
                    pe.wait_ge(gated, post.count(H, H))
                    free(use_gate[0], hid_use(moe, 1, 0), (skip_added, post, H, 1))
                    for b in range(TB):
                        for half in range(H):
                            last = nc.tensor.matmul(bank[0][:, b * C:(b + 1) * C], yg[:, half, b * P:(b + 1) * P],
                                                    w_out[:, half, :], start=(half == 0), stop=(half == H - 1))
                    last.then_inc(attn_projected, 1)
                expert(moe, 1)
                pair_b(i, 3)
                sum_states(i, 2)
                hidden(moe, 2, 0, [use_attn, use_gate[0], hid_use(moe, 1, 0)])
                hidden(moe, 2, 1, [use_gate[1], hid_use(moe, 1, 1)])
                pair_c(i, 3)
                hidden(moe, 3, 0, [hid_use(moe, 2, 0)])
                hidden(moe, 3, 1, [hid_use(moe, 2, 1)])
                if there(pre):
                    pe.wait_ge(u_ready, pre.count(H, H))
                    free(hid_use(moe, 3, 0), use_attn, use_gate[0])
                    for half in range(H):
                        last = nc.tensor.matmul(bank[0][:, :], w_bc[:, half, :], u[:, pre.odd, half, :],
                                                start=(half == 0), stop=(half == H - 1))
                    last.then_inc(bcd_projected, 1)
                pair_b(i, 4)
                sum_states(i, 3)
                expert(moe, 2)
                pair_c(i, 4)
                if there(post):
                    pe.wait_ge(xn_ready[1], post.count(1, 1))
                    free(hid_use(moe, 3, 1), use_gate[1], use_y1)
                    turn(bank[1], xn[:, 1], xn2_turned)
                if there(i):
                    pe.wait_ge(yT_ready, i.count(H, 1))
                    free(use_bcd, hid_use(moe, 3, 0), use_attn)
                    turn(bank[0], yT, y_turned)
                expert(moe, 3)
                pair_b(i, 5)
                sum_states(i, 4)
                if there(pre):
                    pe.wait_ge(bcd_ready, pre.count(1, 1))
                    for half in range(H):
                        free(*([use_y0, use_bcd] if half == 0 else [use_x2T, use_gate[1]]))
                        rows = slice(3 * SPLIT, 3 * SPLIT + RANK)
                        nc.tensor.matmul(bank[half][:, :], w_dt[rows, half * P:(half + 1) * P], bcd[rows, :],
                                         start=True, stop=True).then_inc(dt_projected, 1)
                hidden(moe, 4, 0, [use_dt[0], use_y0, hid_use(moe, 3, 0)])
                hidden(moe, 4, 1, [use_dt[1], use_x2T, hid_use(moe, 3, 1)])
                pair_c(i, 5)
                hidden(moe, 5, 0, [hid_use(moe, 4, 0)])
                hidden(moe, 5, 1, [hid_use(moe, 4, 1)])
                if there(post):
                    pe.wait_ge(x2T_ready, post.count(1, 1))
                    free(hid_use(moe, 5, 1), use_dt[1], use_x2T)
                    for b in range(TB):
                        last = nc.tensor.matmul(bank[1][:, b * E:(b + 1) * E], x2T[:, post.odd, b * P:(b + 1) * P],
                                                gate_w[:, :], start=True, stop=True)
                    last.then_inc(scored, 1)
                pair_b(i, 6)
                sum_states(i, 5)
                expert(moe, 4)
                pair_c(i, 6)
                expert(moe, 5)
                pair_b(i, 7)
                sum_states(i, 6)
                hidden(moe, 6, 0, [hid_use(moe, 5, 0)])
                hidden(moe, 6, 1, [use_scores, hid_use(moe, 5, 1)])
                pair_c(i, 7)
                hidden(moe, 7, 0, [hid_use(moe, 6, 0)])
                hidden(moe, 7, 1, [hid_use(moe, 6, 1)])
                pair_b(pre, 0)

            def pair_b(j, c):
                for q in range(PU // 2):
                    pair(j, c, q)

            def pair_c(j, c):
                for q in range(PU // 2, PU):
                    pair(j, c, q)

            pe.wait_ge(constants_ready, CONSTANTS)
            pe.wait_ge(weights_loaded, 16 * LOADS)
            run(pe, round_, -1, rounds + 2, 3, rounds - 2)


_INS = ['x', 'W_in', 'conv_w', 'conv_b', 'W_x', 'W_dt', 'b_dt', 'A_log', 'D', 'W_out']


def kernel(**inputs):
    import numpy as _np
    import concourse.bacc as _bacc
    from concourse import mybir as _mybir
    from concourse.bass_utils import run_bass_kernel_spmd as _run

    host = {name: inputs[f"L0_attn_{name}"] for name in _INS}
    for name in ("conv_b", "b_dt", "D"):
        host[name] = _np.asarray(host[name]).reshape(H, P).T
    w1, w2 = _np.asarray(inputs["L0_ffn_w1"]), _np.asarray(inputs["L0_ffn_w2"])
    host["gate_wT"] = _np.asarray(inputs["L0_ffn_gate_w"]).T
    host["w1T"] = w1.reshape(-1, w1.shape[2]).T
    host["w2T"] = w2.transpose(2, 0, 1)

    nc = _bacc.Bacc("TRN2", target_bir_lowering=False, num_devices=1)
    arrays, args = {}, []
    for name, a in host.items():
        a = _np.ascontiguousarray(a)
        arrays[f"in_{name}"] = a
        args.append(nc.dram_tensor(f"in_{name}", a.shape, _mybir.dt.from_np(a.dtype), kind="ExternalInput").ap())
    shape = tuple(host["x"].shape)
    args.append(nc.dram_tensor("out_0", shape, _mybir.dt.float32, kind="ExternalOutput").ap())
    mamba_moe(nc, *args)
    r = _run(nc, [arrays], core_ids=[0])
    return r.results[0]["out_0"]
```

```python
from contextlib import ExitStack

import concourse.bass as bass
from concourse import mybir

ALU = mybir.AluOpType
ACT = mybir.ActivationFunctionType
F32 = mybir.dt.float32
BF16 = mybir.dt.bfloat16
U32 = mybir.dt.uint32

P = 128
SEQ = 256
SEQS = 2
T = SEQS * SEQ
TB = T // P
C = 128
H = 2
NS = 16
RING = 4
GROUP = 2
CH = NS // GROUP
RANK = 8
TAPS = 4
E = 8
FH = 2
SPLIT = 32
EPS = 1e-5


class Round:

    def __init__(self, at, loop=None):
        self.at, self.loop = at, loop
        self.odd = at % 2

    def later(self, k):
        return Round(self.at + k, self.loop)

    def count(self, per, more):
        v = self.at * per + more
        return v if self.loop is None else self.loop * (2 * per) + v

    def turn(self, per, more):
        v = self.at // 2 * per + more
        return v if self.loop is None else self.loop * per + v

    def number(self):
        return self.at if self.loop is None else self.loop * 2 + self.at


def mamba_moe(nc, x, W_in, conv_w, conv_b, W_x, W_dt, b_dt, A_log, D, W_out, gate_wT, w1T, w2T, out):
    rounds = x.shape[0] * x.shape[1] // T
    x_v = x.rearrange("(i s) (b p) c -> i p (s b) c", s=SEQS, p=P)
    out_v = out.rearrange("(i s) (b p) c -> i p (s b) c", s=SEQS, p=P)

    def there(*js):
        return all(j.loop is not None or 0 <= j.at < rounds for j in js)

    def wait(eng, sem, value):
        if not isinstance(value, int) or value > 0:
            eng.wait_ge(sem, value)

    def run(eng, body, first, last, loop_first, loop_last):
        for i in range(first, loop_first):
            body(Round(i))
        pairs = (loop_last - loop_first + 1) // 2
        with eng.Fori(0, pairs) as it:
            body(Round(loop_first, it))
            body(Round(loop_first + 1, it))
        for i in range(loop_first + 2 * pairs, last + 1):
            body(Round(i))

    with ExitStack() as ctx:
        def sb(name, shape, dt=F32):
            return ctx.enter_context(nc.sbuf_tensor(name, shape, dt))

        def ps(name, shape):
            return ctx.enter_context(nc.psum_tensor(name, shape, F32))

        def sem(name):
            return ctx.enter_context(nc.semaphore(name))

        w_in = sb("w_in", [P, 4 * P])
        w_bc = sb("w_bc", [P, H, P])
        w_dt = sb("w_dt", [P, H * P])
        w_out = sb("w_out", [P, H, C])
        taps_w = sb("taps_w", [P, H, TAPS])
        conv_bias = sb("conv_bias", [P, H])
        dt_bias = sb("dt_bias", [P, H])
        skip_w = sb("skip_w", [P, H])
        a_neg = sb("a_neg", [P, H, NS])
        gate_w = sb("gate_w", [C, E])
        w1 = sb("w1", [C, E, FH, P])
        w2 = sb("w2", [P, FH, E, C])
        ident = sb("ident", [P, P])
        one_hot = sb("one_hot", [3 * SPLIT, 2 * NS], BF16)
        select = sb("select", [3 * SPLIT, 2 * NS, P], BF16)
        expert_no = sb("expert_no", [P, E])
        power = sb("power", [P, TB])
        x_in = sb("x_in", [P, 2, TB, C])
        stats = sb("stats", [P, 2, TB, 6])
        moments = sb("moments", [P, 2, 3, TB])
        mean = sb("mean", [P, 2, TB])
        variance = sb("variance", [P, 2, TB])
        rstd = sb("rstd", [P, 2, TB])
        xn = sb("xn", [P, 2, TB, C])
        xnT = sb("xnT", [C, T])
        tap = sb("tap", [P, H, TAPS, SEQS, TAPS - 1 + SEQ])
        u = sb("u", [P, 2, H, T])
        gate = sb("gate", [P, 2, H, T])
        bcd = sb("bcd", [P, T])
        rest = sb("rest", [3 * SPLIT, T])
        mid = sb("mid", [3 * SPLIT, T], BF16)
        parts = sb("parts", [3 * SPLIT, 2, T], BF16)
        soft = sb("soft", [P, H, T])
        delta = sb("delta", [P, H, T])
        du = sb("du", [P, 2, H, T])
        dA = sb("dA", [P, 4, H, GROUP, T])
        h = sb("h", [P, RING, H, GROUP, T])
        c_rows = sb("c_rows", [P, 2, T])
        yT = sb("yT", [P, H, TB, P])
        yg = yT.rearrange("p h b t -> p h (b t)")
        x_again = sb("x_again", [P, 2, TB, C])
        x1 = sb("x1", [P, 2, TB, C])
        x2T = sb("x2T", [C, 2, T])
        scores = sb("scores", [P, TB, E])
        top = sb("top", [P, TB, 8])
        top_at = sb("top_at", [P, TB, 8], U32)
        top_no = sb("top_no", [P, TB, 2])
        ratio = sb("ratio", [P, TB])
        prob = sb("prob", [P, 3, TB])
        picked = sb("picked", [P, 2, TB, E])
        cw = sb("cw", [P, 2, TB, E])
        hid = sb("hid", [P, 2, FH, T])
        weighted = sb("weighted", [P, 2, TB, C])

        row_ps = [ps(f"row_ps{k}", [P, T]) for k in range(3)]
        y_ps = ps("y_ps", [P, H, TB, P])
        expert_ps = ps("expert_ps", [P, TB, C])
        bank = [ps("bank0", [P, T]), ps("bank1", [P, T])]

        weights_loaded = sem("weights_loaded")
        late_weights_loaded = sem("late_weights_loaded")
        one_hot_ready = sem("one_hot_ready")
        select_ready = sem("select_ready")
        zeros_set = sem("zeros_set")
        constants_ready = sem("constants_ready")
        a_exp_ready = sem("a_exp_ready")
        a_ready = sem("a_ready")
        x_loaded = [sem("x_loaded0"), sem("x_loaded1")]
        x_again_loaded = [sem("x_again_loaded0"), sem("x_again_loaded1")]
        out_stored = [sem("out_stored0"), sem("out_stored1")]
        stats_ready = [sem("stats_ready0"), sem("stats_ready1")]
        moments_ready = [sem("moments_ready0"), sem("moments_ready1")]
        variance_ready = [sem("variance_ready0"), sem("variance_ready1")]
        rstd_ready = [sem("rstd_ready0"), sem("rstd_ready1")]
        xn_ready = [sem("xn_ready0"), sem("xn_ready1")]
        xn_turned = sem("xn_turned")
        xnT_ready = sem("xnT_ready")
        projected = sem("projected")
        taps_ready = sem("taps_ready")
        gate_ready = sem("gate_ready")
        conv_added = sem("conv_added")
        u_ready = sem("u_ready")
        bcd_projected = sem("bcd_projected")
        bcd_ready = sem("bcd_ready")
        high_ready = sem("high_ready")
        split_step = sem("split_step")
        dt_projected = sem("dt_projected")
        dt_read = sem("dt_read")
        soft_exp = sem("soft_exp")
        soft_ready = sem("soft_ready")
        delta_ready = sem("delta_ready")
        du_ready = sem("du_ready")
        b_ready = sem("b_ready")
        c_ready = sem("c_ready")
        c_first_ready = sem("c_first_ready")
        dA_ready = sem("dA_ready")
        b_used = sem("b_used")
        scan_done = sem("scan_done")
        c_copied = sem("c_copied")
        c_first_used = sem("c_first_used")
        c_used = sem("c_used")
        y_added = sem("y_added")
        yT_ready = sem("yT_ready")
        y_turned = sem("y_turned")
        skip_added = sem("skip_added")
        gated = sem("gated")
        attn_projected = sem("attn_projected")
        x1_ready = sem("x1_ready")
        xn2_turned = sem("xn2_turned")
        x2T_ready = sem("x2T_ready")
        scored = sem("scored")
        scores_ready = sem("scores_ready")
        top_ready = sem("top_ready")
        top_gap = sem("top_gap")
        top_at_ready = sem("top_at_ready")
        ratio_ready = sem("ratio_ready")
        routing_step = sem("routing_step")
        hid_projected = sem("hid_projected")
        hid_ready = sem("hid_ready")
        expert_done = sem("expert_done")
        expert_weighted = sem("expert_weighted")
        expert_added = sem("expert_added")

        LOADS = 11
        LATE_LOADS = 4
        CONSTANTS = 6 + E
        block = ctx.enter_context(nc.Block())

        @block.sync
        def _(sp):
            def load(dst, src):
                sp.dma_start(dst, src).then_inc(weights_loaded, 16)

            def load_late(dst, src):
                sp.dma_start(dst, src).then_inc(late_weights_loaded, 16)

            def start_round(i):
                nxt = i.later(3)
                if there(nxt):
                    wait(sp, xn_ready[0], nxt.count(1, -1))
                    sp.dma_start(x_in[:, nxt.odd], x_v[nxt.number()]).then_inc(x_loaded[nxt.odd], 16)
                if there(i):
                    wait(sp, x1_ready, i.count(1, -1))
                    sp.dma_start(x_again[:, i.odd], x_v[i.number()]).then_inc(x_again_loaded[i.odd], 16)
                done = i.later(-3)
                if there(done):
                    wait(sp, expert_added, done.count(E, E))
                    sp.dma_start(out_v[done.number()], x1[:, done.odd]).then_inc(out_stored[done.odd], 16)

            start_round(Round(-3))
            load(skip_w[:, :], D)
            load(w_in[:, :], W_in)
            start_round(Round(-2))
            load(taps_w[:, :, :], conv_w.rearrange("(h p) o k -> p h (o k)", p=P))
            load(conv_bias[:, :], conv_b)
            for part in range(3):
                load(w_bc[:, :, part * SPLIT:(part + 1) * SPLIT],
                     W_x[:, RANK:RANK + 2 * NS].rearrange("(h p) n -> p h n", p=P))
            load(w_bc[:, :, 3 * SPLIT:3 * SPLIT + RANK], W_x[:, 0:RANK].rearrange("(h p) n -> p h n", p=P))
            load(w_dt[3 * SPLIT:3 * SPLIT + RANK, :], W_dt)
            load(dt_bias[:, :], b_dt)
            load(a_neg[:, :, :], A_log.rearrange("(h p) n -> p h n", p=P))
            load_late(w_out[:, :, :], W_out.rearrange("(h p) c -> p h c", p=P))
            load_late(w1[:, :, :, :], w1T.rearrange("c (e h f) -> c e h f", e=E, h=FH))
            load_late(w2[:, :, :, :], w2T.rearrange("(h p) e c -> p h e c", p=P))
            load_late(gate_w[:, :], gate_wT)
            start_round(Round(-1))
            run(sp, start_round, 0, rounds + 2, 3, rounds - 4)
            for odd in range(2):
                sp.wait_ge(out_stored[odd], 16 * (rounds // 2))

        @block.gpsimd
        def _(pool):
            nc.gpsimd.memset(ident[:, :], 0.0).then_inc(zeros_set, 1)
            nc.gpsimd.memset(one_hot[:, :], 0.0).then_inc(zeros_set, 1)
            nc.gpsimd.memset(tap[:, :, 0:TAPS - 1, :, 0:TAPS - 1], 0.0).then_inc(constants_ready, 1)
            nc.gpsimd.memset(dA[:, :, :, :, 0:1], 0.0).then_inc(constants_ready, 1)
            nc.gpsimd.memset(dA[:, :, :, :, SEQ:SEQ + 1], 0.0).then_inc(constants_ready, 1)
            nc.gpsimd.memset(w_bc[:, :, 3 * SPLIT + RANK:], 0.0).then_inc(constants_ready, 1)
            nc.gpsimd.memset(power[:, :], -0.5).then_inc(constants_ready, 1)
            for e in range(E):
                nc.gpsimd.memset(expert_no[:, e:e + 1], float(e)).then_inc(constants_ready, 1)
            pool.wait_ge(zeros_set, 2)
            nc.gpsimd.affine_select(out=ident[:, :], in_=ident[:, :], compare_op=ALU.not_equal, fill=1.0,
                                    base=0, pattern=[[-1, P]], channel_multiplier=1).then_inc(constants_ready, 1)
            pool.wait_ge(constants_ready, 6 + E)
            for part in range(3):
                nc.gpsimd.affine_select(out=one_hot[:, :], in_=one_hot[:, :], compare_op=ALU.not_equal,
                                        fill=1.0, base=-part * SPLIT, pattern=[[-1, 2 * NS]],
                                        channel_multiplier=1).then_inc(one_hot_ready, 1)
                pool.wait_ge(one_hot_ready, part + 1)

            def inverse_deviation(j, k):
                if not there(j):
                    return
                pool.wait_ge(variance_ready[k], j.count(1, 1))
                wait(pool, xn_ready[k], j.count(1, 0))
                nc.gpsimd.tensor_tensor(rstd[:, k, :], variance[:, k, :], power[:, 0:TB],
                                        ALU.pow).then_inc(rstd_ready[k], 1)

            def convolve(j, half):
                if not there(j):
                    return
                total = tap[:, half, TAPS - 1, :, TAPS - 1:]
                for k in range(TAPS - 1):
                    if k == 0:
                        pool.wait_ge(taps_ready, j.count(H, half + 1))
                    else:
                        pool.wait_ge(conv_added, j.count(H * (TAPS - 1), half * (TAPS - 1) + k))
                    nc.gpsimd.tensor_tensor(total, total, tap[:, half, k, :, k:k + SEQ],
                                            ALU.add).then_inc(conv_added, 1)

            def split(j, post, moe):
                if not there(j):
                    return
                odd = j.odd
                pool.wait_ge(conv_added, j.count(H * (TAPS - 1), H * (TAPS - 1)))
                if there(post):
                    pool.wait_ge(rstd_ready[1], post.count(1, 1))
                if there(j.later(-1)):
                    pool.wait_ge(c_used, j.later(-1).count(CH, 4))
                if there(moe):
                    pool.wait_ge(expert_added, moe.count(E, 2))
                pool.wait_ge(high_ready, j.count(1, 1))
                second, third = slice(SPLIT, 2 * SPLIT), slice(2 * SPLIT, 3 * SPLIT)
                nc.gpsimd.tensor_tensor(rest[third, :], bcd[third, :], parts[third, odd, :], ALU.subtract)
                nc.gpsimd.tensor_tensor(mid[third, :], bcd[third, :], parts[third, odd, :],
                                        ALU.subtract).then_inc(split_step, 1)
                pool.wait_ge(split_step, j.count(3, 1))
                nc.gpsimd.tensor_tensor(parts[second, odd, :], bcd[second, :], parts[second, odd, :],
                                        ALU.subtract).then_inc(split_step, 1)
                pool.wait_ge(split_step, j.count(3, 2))
                nc.gpsimd.tensor_tensor(parts[third, odd, :], rest[third, :], mid[third, :],
                                        ALU.subtract).then_inc(split_step, 1)
                pool.wait_ge(split_step, j.count(3, 3))

            def add_soft(j):
                if not there(j):
                    return
                odd = j.odd
                pool.wait_ge(soft_ready, j.count(1, 1))
                nc.gpsimd.tensor_tensor(delta[:, :, :], delta[:, :, :], soft[:, :, :], ALU.add).then_inc(delta_ready, 1)
                pool.wait_ge(delta_ready, j.count(1, 1))
                pool.wait_ge(u_ready, j.count(H, H))
                wait(pool, b_used, j.count(CH * GROUP, -CH * GROUP))
                nc.gpsimd.tensor_tensor(du[:, odd], delta[:, :, :], u[:, odd], ALU.mult).then_inc(du_ready, 1)

            def outputs(j, c):
                if not there(j):
                    return
                pool.wait_ge(c_copied, j.count(CH, c + 1))
                pool.wait_ge(scan_done, j.count(CH, c + 1))
                at = h[:, c % RING, :, 1, :]
                nc.gpsimd.tensor_tensor(at, at, c_rows[:, c % 2, :].unsqueeze(1).broadcast_to([P, H, T]),
                                        ALU.mult).then_inc(c_used, 1)

            def add_expert(j, e):
                if not there(j):
                    return
                pool.wait_ge(expert_weighted, j.count(E, e + 1))
                wait(pool, expert_added, j.count(E, e))
                nc.gpsimd.tensor_tensor(x1[:, j.odd], x1[:, j.odd], weighted[:, e % 2],
                                        ALU.add).then_inc(expert_added, 1)

            def round_(i):
                pre, post, moe, old = (i.later(k) for k in (1, -1, -2, -3))
                convolve(pre, 0)
                outputs(i, 0)
                add_expert(old, E - 2)
                convolve(pre, 1)
                outputs(i, 1)
                add_expert(old, E - 1)
                outputs(i, 2)
                add_expert(moe, 0)
                outputs(i, 3)
                add_expert(moe, 1)
                inverse_deviation(post, 1)
                split(pre, post, moe)
                outputs(i, 4)
                add_expert(moe, 2)
                inverse_deviation(i.later(2), 0)
                outputs(i, 5)
                add_soft(pre)
                add_expert(moe, 3)
                outputs(i, 6)
                add_expert(moe, 4)
                outputs(i, 7)
                add_expert(moe, 5)

            run(pool, round_, -2, rounds + 2, 3, rounds - 3)

        @block.scalar
        def _(act):
            act.wait_ge(weights_loaded, 16 * LOADS)
            act.wait_ge(constants_ready, CONSTANTS)
            nc.scalar.activation(a_neg[:, :, :], a_neg[:, :, :], ACT.Exp).then_inc(a_exp_ready, 1)

            def decay(j, c):
                if not there(j):
                    return
                if c == 0:
                    act.wait_ge(delta_ready, j.count(1, 1))
                wait(act, scan_done, j.count(CH, c - 3))
                for half in range(H):
                    src = delta[:, half, :].rearrange("p (s t) -> p s t", s=SEQS)[:, :, 1:SEQ]
                    for n in range(GROUP):
                        dst = dA[:, c % 4, half, n, :].rearrange("p (s t) -> p s t", s=SEQS)[:, :, 1:SEQ]
                        k = c * GROUP + n
                        last = nc.scalar.activation(dst, src, ACT.Exp, scale=a_neg[:, half, k:k + 1])
                last.then_inc(dA_ready, 1)

            def copy_c(j, c):
                if not there(j):
                    return
                act.wait_ge(c_ready, j.count(CH, c + 1))
                wait(act, c_used, j.count(CH, c - 1))
                nc.scalar.activation(c_rows[:, c % 2, :], row_ps[2][:, :], ACT.Copy).then_inc(c_copied, 1)

            def copy_y(j):
                if not there(j):
                    return
                act.wait_ge(y_added, j.count(CH, CH))
                wait(act, attn_projected, j.count(1, 0))
                nc.scalar.activation(yT[:, :, :, :], y_ps[:, :, :, :], ACT.Copy).then_inc(yT_ready, 1)

            def hidden(j, e):
                if not there(j):
                    return
                wait(act, expert_done, j.count(E, e - 1))
                for f in range(FH):
                    act.wait_ge(hid_projected, j.count(E * FH, FH * e + f + 1))
                    nc.scalar.activation(hid[:, e % 2, f, :], bank[f][:, :], ACT.Silu).then_inc(hid_ready, 1)

            def taps(j, half):
                if not there(j):
                    return
                wait(act, conv_added, j.count(H * (TAPS - 1), 0))
                act.wait_ge(projected, j.count(2 * H, half + 1))
                for k in range(TAPS):
                    last = nc.scalar.activation(tap[:, half, k, :, TAPS - 1:],
                                                bank[half][:, :].rearrange("p (s t) -> p s t", s=SEQS),
                                                ACT.Copy, scale=taps_w[:, half, k:k + 1])
                last.then_inc(taps_ready, 1)

            def activations(j):
                if not there(j):
                    return
                wait(act, gated, j.count(1, -1))
                for half in range(H):
                    act.wait_ge(projected, j.count(2 * H, H + half + 1))
                    nc.scalar.activation(gate[:, j.odd, half, :], bank[half][:, :], ACT.Silu).then_inc(gate_ready, 1)
                for half in range(H):
                    act.wait_ge(conv_added, j.count(H * (TAPS - 1), (half + 1) * (TAPS - 1)))
                    nc.scalar.activation(u[:, j.odd, half, :].rearrange("p (s t) -> p s t", s=SEQS),
                                         tap[:, half, TAPS - 1, :, TAPS - 1:], ACT.Silu,
                                         bias=conv_bias[:, half:half + 1]).then_inc(u_ready, 1)

            def copy_bcd(j):
                if not there(j):
                    return
                act.wait_ge(bcd_projected, j.count(1, 1))
                wait(act, split_step, j.count(3, 0))
                wait(act, dt_projected, j.count(H, 0))
                nc.scalar.activation(bcd[0:3 * SPLIT + RANK, :], bank[0][0:3 * SPLIT + RANK, :],
                                     ACT.Copy).then_inc(bcd_ready, 1)
                wait(act, c_first_ready, j.count(CH, -CH))
                nc.scalar.activation(parts[:, j.odd, :], bank[0][0:3 * SPLIT, :], ACT.Copy).then_inc(high_ready, 1)

            def soft_parts(j):
                if not there(j):
                    return
                wait(act, du_ready, j.count(1, 0))
                wait(act, dA_ready, j.count(CH, 0))
                for half in range(H):
                    act.wait_ge(dt_projected, j.count(H, half + 1))
                    nc.scalar.activation(soft[:, half, :], bank[half][:, :], ACT.Abs,
                                         bias=dt_bias[:, half:half + 1])
                    nc.scalar.activation(delta[:, half, :], bank[half][:, :], ACT.Relu,
                                         bias=dt_bias[:, half:half + 1]).then_inc(dt_read, 1)

            def soft_exp_(j):
                if not there(j):
                    return
                act.wait_ge(dt_read, j.count(H, H))
                nc.scalar.activation(soft[:, :, :], soft[:, :, :], ACT.Exp, scale=-1.0).then_inc(soft_exp, 1)

            def soft_log(j):
                if not there(j):
                    return
                act.wait_ge(soft_exp, j.count(1, 1))
                nc.scalar.activation(soft[:, :, :], soft[:, :, :], ACT.Ln, bias=1.0).then_inc(soft_ready, 1)

            def copy_x2T(j):
                if not there(j):
                    return
                act.wait_ge(xn2_turned, j.count(1, 1))
                wait(act, hid_projected, j.count(E * FH, -E * FH))
                nc.scalar.activation(x2T[:, j.odd, :], bank[1][:, :], ACT.Copy).then_inc(x2T_ready, 1)

            def copy_xnT(j):
                if not there(j):
                    return
                act.wait_ge(xn_turned, j.count(1, 1))
                wait(act, projected, j.count(2 * H, 0))
                nc.scalar.activation(xnT[:, :], bank[0][:, :], ACT.Copy).then_inc(xnT_ready, 1)

            def ratio_exp(j):
                if not there(j):
                    return
                act.wait_ge(top_gap, j.count(1, 1))
                nc.scalar.activation(ratio[:, :], ratio[:, :], ACT.Exp).then_inc(ratio_ready, 1)

            def round_(i):
                ahead, pre, post, moe = (i.later(k) for k in (2, 1, -1, -2))
                ratio_exp(moe)
                decay(i, 2)
                copy_c(i, 0)
                taps(pre, 1)
                decay(i, 3)
                copy_c(i, 1)
                copy_y(post)
                hidden(moe, 0)
                hidden(moe, 1)
                decay(i, 4)
                copy_c(i, 2)
                decay(i, 5)
                activations(pre)
                copy_c(i, 3)
                hidden(moe, 2)
                hidden(moe, 3)
                copy_bcd(pre)
                decay(i, 6)
                copy_c(i, 4)
                decay(i, 7)
                soft_parts(pre)
                copy_c(i, 5)
                soft_exp_(pre)
                copy_x2T(post)
                hidden(moe, 4)
                hidden(moe, 5)
                soft_log(pre)
                copy_c(i, 6)
                decay(pre, 0)
                copy_xnT(ahead)
                decay(pre, 1)
                taps(ahead, 0)
                copy_c(i, 7)
                hidden(moe, 6)
                hidden(moe, 7)

            act.wait_ge(a_ready, 1)
            run(act, round_, -2, rounds + 1, 3, rounds - 3)

        @block.vector
        def _(dve):
            def inputs(j, c):
                if c == 0:
                    dve.wait_ge(du_ready, j.count(1, 1))
                wait(dve, y_added, j.count(CH, c + 1 - RING))
                for n in range(GROUP):
                    dve.wait_ge(b_ready, j.count(CH * GROUP, c * GROUP + n + 1))
                    nc.vector.tensor_tensor(h[:, c % RING, :, n, :], du[:, j.odd],
                                            row_ps[n][:, :].unsqueeze(1).broadcast_to([P, H, T]),
                                            ALU.mult).then_inc(b_used, 1)

            def scan(j, c):
                dve.wait_ge(b_used, j.count(CH * GROUP, c * GROUP + GROUP))
                dve.wait_ge(dA_ready, j.count(CH, c + 1))
                run_ = h[:, c % RING].rearrange("p h n t -> p (h n t)")
                nc.vector.tensor_tensor_scan(run_, dA[:, c % 4].rearrange("p h n t -> p (h n t)"), run_, 0.0,
                                             ALU.mult, ALU.add).then_inc(scan_done, 1)

            def outputs(j, c):
                dve.wait_ge(c_first_ready, j.count(CH, c + 1))
                dve.wait_ge(scan_done, j.count(CH, c + 1))
                at = h[:, c % RING, :, 0, :]
                nc.vector.tensor_tensor(at, at, row_ps[2][:, :].unsqueeze(1).broadcast_to([P, H, T]),
                                        ALU.mult).then_inc(c_first_used, 1)

            def norm_stats(j, k, src):
                for b in range(TB):
                    last = nc.vector.bn_stats(stats[:, k, b, :], src[:, b, :])
                last.then_inc(stats_ready[k], 1)
                even, odd = ([stats[:, k, :, 3 * o + v] for v in (1, 2)] for o in range(2))
                total, gap, spread = (moments[:, k, v, :] for v in range(3))
                dve.wait_ge(stats_ready[k], j.count(1, 1))
                nc.vector.tensor_tensor(total, even[0], odd[0], ALU.add)
                nc.vector.tensor_tensor(gap, even[0], odd[0], ALU.subtract)
                nc.vector.tensor_tensor(spread, even[1], odd[1], ALU.add).then_inc(moments_ready[k], 1)
                dve.wait_ge(moments_ready[k], j.count(3, 1))
                nc.vector.tensor_scalar(mean[:, k, :], total, 0.5, None, ALU.mult)
                nc.vector.scalar_tensor_tensor(out=gap, in0=gap, scalar=C / 4, in1=gap, op0=ALU.mult,
                                               op1=ALU.mult).then_inc(moments_ready[k], 1)
                dve.wait_ge(moments_ready[k], j.count(3, 2))
                nc.vector.tensor_tensor(spread, spread, gap, ALU.add).then_inc(moments_ready[k], 1)
                dve.wait_ge(moments_ready[k], j.count(3, 3))
                nc.vector.tensor_scalar(variance[:, k, :], spread, 1.0 / C, EPS, ALU.mult,
                                        ALU.add).then_inc(variance_ready[k], 1)

            def norm_apply(j, k, src, turned):
                dve.wait_ge(rstd_ready[k], j.count(1, 1))
                wait(dve, turned, j.count(1, 0))
                for b in range(TB):
                    last = nc.vector.tensor_scalar(xn[:, k, b, :], src[:, b, :], mean[:, k, b:b + 1],
                                                   rstd[:, k, b:b + 1], ALU.subtract, ALU.mult)
                last.then_inc(xn_ready[k], 1)

            def pre_stats(j):
                if there(j):
                    dve.wait_ge(x_loaded[j.odd], j.turn(16, 16))
                    norm_stats(j, 0, x_in[:, j.odd])

            def pre_norm(j):
                if there(j):
                    norm_apply(j, 0, x_in[:, j.odd], xn_turned)

            def add_skip(j):
                if not there(j):
                    return
                dve.wait_ge(y_turned, j.count(H, H))
                for half in range(H):
                    nc.vector.scalar_tensor_tensor(out=yg[:, half, :], in0=u[:, j.odd, half, :],
                                                   scalar=skip_w[:, half:half + 1], in1=bank[half][:, :],
                                                   op0=ALU.mult, op1=ALU.add).then_inc(skip_added, 1)

            def gating(j):
                if not there(j):
                    return
                dve.wait_ge(skip_added, j.count(H, H))
                dve.wait_ge(gate_ready, j.count(H, H))
                nc.vector.tensor_tensor(yg[:, :, :], yg[:, :, :], gate[:, j.odd], ALU.mult).then_inc(gated, 1)

            def residual(j):
                if there(j):
                    dve.wait_ge(attn_projected, j.count(1, 1))
                    dve.wait_ge(x_again_loaded[j.odd], j.turn(16, 16))
                    wait(dve, out_stored[j.odd], j.turn(16, 0))
                    nc.vector.tensor_tensor(x1[:, j.odd], x_again[:, j.odd],
                                            bank[0][:, :].rearrange("p (b c) -> p b c", b=TB),
                                            ALU.add).then_inc(x1_ready, 1)

            def post_stats(j):
                if there(j):
                    dve.wait_ge(x1_ready, j.count(1, 1))
                    norm_stats(j, 1, x1[:, j.odd])

            def post_norm(j):
                if there(j):
                    norm_apply(j, 1, x1[:, j.odd], xn2_turned)

            def top_two(j):
                if not there(j):
                    return
                dve.wait_ge(scored, j.count(1, 1))
                in_bank = bank[1][:, 0:TB * E].rearrange("p (b e) -> p b e", b=TB)
                nc.vector.tensor_copy(scores[:, :, :], in_bank).then_inc(scores_ready, 1)
                for b in range(TB):
                    last = nc.vector.max(out=top[:, b, :], in_=in_bank[:, b, :])
                last.then_inc(top_ready, 1)
                dve.wait_ge(scores_ready, j.count(1, 1))
                dve.wait_ge(top_ready, j.count(1, 1))
                nc.vector.tensor_tensor(ratio[:, :], top[:, :, 1], top[:, :, 0], ALU.subtract).then_inc(top_gap, 1)
                for b in range(TB):
                    last = nc.vector.max_index(top_at[:, b, :], top[:, b, :], scores[:, b, :])
                last.then_inc(top_at_ready, 1)

            def routing(j):
                if not there(j):
                    return
                step = 0

                def then(ins):
                    nonlocal step
                    step += 1
                    ins.then_inc(routing_step, 1)

                def so_far():
                    dve.wait_ge(routing_step, j.count(8, step))

                dve.wait_ge(ratio_ready, j.count(1, 1))
                dve.wait_ge(top_at_ready, j.count(1, 1))
                then(nc.vector.tensor_scalar(prob[:, 0, :], ratio[:, :], 1.0, None, ALU.add))
                then(nc.vector.tensor_copy(top_no[:, :, :], top_at[:, :, 0:2]))
                so_far()
                then(nc.vector.reciprocal(prob[:, 1, :], prob[:, 0, :]))
                for k in range(2):
                    no = top_no[:, :, k:k + 1].broadcast_to([P, TB, E])
                    then(nc.vector.tensor_tensor(picked[:, k], expert_no[:, :].unsqueeze(1).broadcast_to([P, TB, E]),
                                                 no, ALU.is_equal))
                so_far()
                nc.vector.tensor_tensor(prob[:, 2, :], ratio[:, :], prob[:, 1, :], ALU.mult).then_inc(routing_step, 1)
                step += 1
                so_far()
                for k in range(2):
                    pk = prob[:, 1 + k, :].unsqueeze(2).broadcast_to([P, TB, E])
                    last = nc.vector.tensor_tensor(picked[:, k], picked[:, k], pk, ALU.mult)
                then(last)
                so_far()
                then(nc.vector.tensor_tensor(cw[:, j.odd], picked[:, 0], picked[:, 1], ALU.add))

            def weight_expert(j, e):
                if not there(j):
                    return
                dve.wait_ge(expert_done, j.count(E, e + 1))
                if e == 0:
                    dve.wait_ge(routing_step, j.count(8, 8))
                wait(dve, expert_added, j.count(E, e - 1))
                nc.vector.tensor_tensor(weighted[:, e % 2], expert_ps[:, :, :],
                                        cw[:, j.odd, :, e:e + 1].broadcast_to([P, TB, C]),
                                        ALU.mult).then_inc(expert_weighted, 1)

            def round_(i):
                ahead, post, moe, old = i.later(2), i.later(-1), i.later(-2), i.later(-3)
                for c in range(CH):
                    if there(i):
                        inputs(i, c)
                    before = (post, CH - 1) if c == 0 else (i, c - 1)
                    if there(before[0]):
                        outputs(*before)
                    if there(i):
                        scan(i, c)
                    if c == 2:
                        add_skip(post)
                        gating(post)
                    if c == 3:
                        residual(post)
                    weight_expert(*((old, E - 2 + c) if c < 2 else (moe, c - 2)))
                    if c == 0:
                        routing(moe)
                    if c == 3:
                        post_stats(post)
                    if c == 4:
                        post_norm(post)
                        pre_stats(ahead)
                    if c == 5:
                        pre_norm(ahead)
                    if c == 6:
                        top_two(post)

            dve.wait_ge(one_hot_ready, 3)
            nc.vector.tensor_copy(select[:, :, :], one_hot[:, :].unsqueeze(2).broadcast_to([3 * SPLIT, 2 * NS, P])
                                  ).then_inc(select_ready, 1)
            dve.wait_ge(constants_ready, CONSTANTS)
            dve.wait_ge(weights_loaded, 16 * LOADS)
            dve.wait_ge(a_exp_ready, 1)
            nc.vector.tensor_scalar(a_neg[:, :, :], a_neg[:, :, :], -1.0, None, ALU.mult).then_inc(a_ready, 1)
            run(dve, round_, -2, rounds + 2, 3, rounds - 3)

        @block.tensor
        def _(pe):
            def free(*uses):
                for s, j, per, more in uses:
                    if there(j):
                        pe.wait_ge(s, j.count(per, more))
                        return

            def broadcast(dst, j, row, ready):
                nc.tensor.matmul(dst[:, :], select[:, row, :], parts[:, j.odd, :], start=True,
                                 stop=True).then_inc(ready, 1)

            def rows_b(j, c):
                if not there(j):
                    return
                if c == 0:
                    pe.wait_ge(split_step, j.count(3, 3))
                for n in range(GROUP):
                    wait(pe, b_used, j.count(CH * GROUP, (c - 1) * GROUP + n + 1))
                    broadcast(row_ps[n], j, c * GROUP + n, b_ready)

            def row_c(j, c):
                if not there(j):
                    return
                wait(pe, c_first_used, j.count(CH, c))
                broadcast(row_ps[2], j, NS + c * GROUP + 1, c_ready)

            def row_c_first(j, c):
                if not there(j):
                    return
                pe.wait_ge(c_copied, j.count(CH, c + 1))
                broadcast(row_ps[2], j, NS + c * GROUP, c_first_ready)

            def sum_states(j, c):
                if not there(j):
                    return
                pe.wait_ge(c_first_used, j.count(CH, c + 1))
                pe.wait_ge(c_used, j.count(CH, c + 1))
                if c == 0:
                    wait(pe, yT_ready, j.count(1, 0))
                for half in range(H):
                    for n in range(GROUP):
                        for b in range(TB):
                            last = nc.tensor.matmul(y_ps[:, half, b, :], h[:, c % RING, half, n, b * P:(b + 1) * P],
                                                    ident[:, :], is_transpose=True,
                                                    start=(c == 0 and n == 0 and b == 0),
                                                    stop=(c == CH - 1 and n == GROUP - 1), skip_group_check=True)
                last.then_inc(y_added, 1)

            def turn(dst, src, signal):
                for b in range(TB):
                    last = nc.tensor.transpose(dst[:, b * P:(b + 1) * P], src[:, b, :], ident[:, :])
                last.then_inc(signal, 1)

            def hidden(j, e, f, uses):
                if not there(j):
                    return
                if e == 0 and f == 0:
                    pe.wait_ge(x2T_ready, j.count(1, 1))
                free(*uses)
                nc.tensor.matmul(bank[f][:, :], w1[:, e, f, :], x2T[:, j.odd, :], start=True,
                                 stop=True).then_inc(hid_projected, 1)

            def expert(j, e):
                if not there(j):
                    return
                pe.wait_ge(hid_ready, j.count(E * FH, FH * (e + 1)))
                wait(pe, expert_weighted, j.count(E, e))
                for b in range(TB):
                    for f in range(FH):
                        last = nc.tensor.matmul(expert_ps[:, b, :], hid[:, e % 2, f, b * P:(b + 1) * P],
                                                w2[:, f, e, :], start=(f == 0), stop=(f == FH - 1))
                last.then_inc(expert_done, 1)

            def round_(i):
                ahead, pre, post, moe, old = (i.later(k) for k in (2, 1, -1, -2, -3))

                def use_hid(j, e, f):
                    return (hid_ready, j, E * FH, FH * e + f + 1)

                use_xi0, use_xi1 = (taps_ready, ahead, H, 1), (taps_ready, pre, H, 2)
                use_y = [(skip_added, post, H, f + 1) for f in range(H)]
                use_gate = [(gate_ready, pre, H, f + 1) for f in range(H)]
                use_attn = (x1_ready, post, 1, 1)
                use_bcd = (high_ready, pre, 1, 1)
                use_dt = [(dt_read, pre, H, f + 1) for f in range(H)]
                use_x2T = (x2T_ready, post, 1, 1)
                use_scores = (top_ready, post, 1, 1)
                use_xnT = (xnT_ready, ahead, 1, 1)
                past_xi = (taps_ready, pre, H, 1)
                past_dt = (dt_read, i, H, 2)
                past_scores = (top_ready, moe, 1, 1)

                def project(j, f, *uses):
                    if not there(j):
                        return
                    if f == 0:
                        pe.wait_ge(xnT_ready, j.count(1, 1))
                    free(*uses)
                    nc.tensor.matmul(bank[f % H][:, :], w_in[:, f * P:(f + 1) * P], xnT[:, :], start=True,
                                     stop=True).then_inc(projected, 1)

                def delta_rank(half, *uses):
                    if not there(pre):
                        return
                    if half == 0:
                        pe.wait_ge(bcd_ready, pre.count(1, 1))
                    free(*uses)
                    rows = slice(3 * SPLIT, 3 * SPLIT + RANK)
                    nc.tensor.matmul(bank[half][:, :], w_dt[rows, half * P:(half + 1) * P], bcd[rows, :],
                                     start=True, stop=True).then_inc(dt_projected, 1)

                expert(old, E - 2)
                rows_b(i, 1)
                row_c(i, 0)
                project(pre, 1, use_hid(old, 7, 1), past_scores, past_dt)
                sum_states(post, 7)
                row_c_first(i, 0)
                expert(old, E - 1)
                rows_b(i, 2)
                row_c(i, 1)
                hidden(moe, 0, 0, [use_hid(old, 7, 0), past_xi])
                hidden(moe, 0, 1, [use_xi1, use_hid(old, 7, 1)])
                row_c_first(i, 1)
                sum_states(i, 0)
                hidden(moe, 1, 0, [use_hid(moe, 0, 0)])
                hidden(moe, 1, 1, [use_hid(moe, 0, 1)])
                rows_b(i, 3)
                row_c(i, 2)
                if there(post):
                    pe.wait_ge(yT_ready, post.count(1, 1))
                    for f in range(H):
                        free(use_hid(moe, 1, f), (past_xi, use_xi1)[f])
                        turn(bank[f], yT[:, f], y_turned)
                expert(moe, 0)
                sum_states(i, 1)
                row_c_first(i, 2)
                project(pre, 2, use_y[0], past_xi)
                project(pre, 3, use_y[1], use_xi1)
                expert(moe, 1)
                rows_b(i, 4)
                row_c(i, 3)
                if there(post):
                    pe.wait_ge(gated, post.count(1, 1))
                    free(use_gate[0], use_y[0])
                    for b in range(TB):
                        for half in range(H):
                            last = nc.tensor.matmul(bank[0][:, b * C:(b + 1) * C], yg[:, half, b * P:(b + 1) * P],
                                                    w_out[:, half, :], start=(half == 0), stop=(half == H - 1))
                    last.then_inc(attn_projected, 1)
                sum_states(i, 2)
                hidden(moe, 2, 0, [use_attn, use_hid(moe, 1, 0)])
                hidden(moe, 2, 1, [use_gate[1], use_y[1], use_hid(moe, 1, 1)])
                row_c_first(i, 3)
                hidden(moe, 3, 0, [use_hid(moe, 2, 0)])
                hidden(moe, 3, 1, [use_hid(moe, 2, 1)])
                if there(pre):
                    pe.wait_ge(u_ready, pre.count(H, H))
                    free(use_hid(moe, 3, 0), use_attn, use_gate[0])
                    for half in range(H):
                        last = nc.tensor.matmul(bank[0][:, :], w_bc[:, half, :], u[:, pre.odd, half, :],
                                                start=(half == 0), stop=(half == H - 1))
                    last.then_inc(bcd_projected, 1)
                expert(moe, 2)
                rows_b(i, 5)
                row_c(i, 4)
                sum_states(i, 3)
                delta_rank(0, use_bcd)
                delta_rank(1, use_hid(moe, 3, 1), use_gate[1])
                row_c_first(i, 4)
                expert(moe, 3)
                rows_b(i, 6)
                row_c(i, 5)
                sum_states(i, 4)
                hidden(moe, 4, 0, [use_dt[0], use_hid(moe, 3, 0)])
                if there(post):
                    pe.wait_ge(xn_ready[1], post.count(1, 1))
                    free(use_dt[1], use_hid(moe, 3, 1))
                    turn(bank[1], xn[:, 1], xn2_turned)
                hidden(moe, 4, 1, [use_x2T, use_hid(moe, 3, 1)])
                row_c_first(i, 5)
                hidden(moe, 5, 0, [use_hid(moe, 4, 0)])
                hidden(moe, 5, 1, [use_hid(moe, 4, 1)])
                expert(moe, 4)
                rows_b(i, 7)
                row_c(i, 6)
                if there(post):
                    pe.wait_ge(x2T_ready, post.count(1, 1))
                    free(use_hid(moe, 5, 1), use_x2T)
                    for b in range(TB):
                        last = nc.tensor.matmul(bank[1][:, b * E:(b + 1) * E], x2T[:, post.odd, b * P:(b + 1) * P],
                                                gate_w[:, :], start=True, stop=True)
                    last.then_inc(scored, 1)
                sum_states(i, 5)
                if there(ahead):
                    pe.wait_ge(xn_ready[0], ahead.count(1, 1))
                    free(use_hid(moe, 5, 0), use_dt[0])
                    turn(bank[0], xn[:, 0], xn_turned)
                row_c_first(i, 6)
                expert(moe, 5)
                project(ahead, 0, use_xnT)
                rows_b(pre, 0)
                row_c(i, 7)
                sum_states(i, 6)
                hidden(moe, 6, 0, [use_xi0, use_hid(moe, 5, 0)])
                hidden(moe, 6, 1, [use_scores, use_hid(moe, 5, 1)])
                row_c_first(i, 7)
                hidden(moe, 7, 0, [use_hid(moe, 6, 0)])
                hidden(moe, 7, 1, [use_hid(moe, 6, 1)])

            pe.wait_ge(constants_ready, CONSTANTS)
            pe.wait_ge(weights_loaded, 16 * LOADS)
            pe.wait_ge(late_weights_loaded, 16 * LATE_LOADS)
            pe.wait_ge(select_ready, 1)
            run(pe, round_, -2, rounds + 2, 3, rounds - 3)


_INS = ['x', 'W_in', 'conv_w', 'conv_b', 'W_x', 'W_dt', 'b_dt', 'A_log', 'D', 'W_out']


def kernel(**inputs):
    import numpy as _np
    import concourse.bacc as _bacc
    from concourse import mybir as _mybir
    from concourse.bass_utils import run_bass_kernel_spmd as _run

    host = {name: inputs[f"L0_attn_{name}"] for name in _INS}
    for name in ("conv_b", "b_dt", "D"):
        host[name] = _np.asarray(host[name]).reshape(H, P).T
    w1, w2 = _np.asarray(inputs["L0_ffn_w1"]), _np.asarray(inputs["L0_ffn_w2"])
    host["gate_wT"] = _np.asarray(inputs["L0_ffn_gate_w"]).T
    host["w1T"] = w1.reshape(-1, w1.shape[2]).T
    host["w2T"] = w2.transpose(2, 0, 1)

    nc = _bacc.Bacc("TRN2", target_bir_lowering=False, num_devices=1)
    arrays, args = {}, []
    for name, a in host.items():
        a = _np.ascontiguousarray(a)
        arrays[f"in_{name}"] = a
        args.append(nc.dram_tensor(f"in_{name}", a.shape, _mybir.dt.from_np(a.dtype), kind="ExternalInput").ap())
    shape = tuple(host["x"].shape)
    args.append(nc.dram_tensor("out_0", shape, _mybir.dt.float32, kind="ExternalOutput").ap())
    mamba_moe(nc, *args)
    r = _run(nc, [arrays], core_ids=[0])
    return r.results[0]["out_0"]
```

```python
from contextlib import ExitStack

import concourse.bass as bass
from concourse import mybir

ALU = mybir.AluOpType
ACT = mybir.ActivationFunctionType
F32 = mybir.dt.float32
BF16 = mybir.dt.bfloat16
U32 = mybir.dt.uint32

P = 128
SEQ = 256
SEQS = 2
T = SEQS * SEQ
TB = T // P
C = 128
H = 2
NS = 16
RING = 4
GROUP = 2
CH = NS // GROUP
RANK = 8
TAPS = 4
E = 8
FH = 2
SPLIT = 32
EPS = 1e-5


class Round:

    def __init__(self, at, loop=None):
        self.at, self.loop = at, loop
        self.odd = at % 2

    def later(self, k):
        return Round(self.at + k, self.loop)

    def count(self, per, more):
        v = self.at * per + more
        return v if self.loop is None else self.loop * (2 * per) + v

    def turn(self, per, more):
        v = self.at // 2 * per + more
        return v if self.loop is None else self.loop * per + v

    def number(self):
        return self.at if self.loop is None else self.loop * 2 + self.at




def mamba_moe(nc, x, W_in, conv_w, conv_b, W_x, W_dt, b_dt, A_log, D, W_out, gate_wT, w1T, w2T, out):
    rounds = x.shape[0] * x.shape[1] // T
    x_v = x.rearrange("(i s) (b p) c -> i p (s b) c", s=SEQS, p=P)
    out_v = out.rearrange("(i s) (b p) c -> i p (s b) c", s=SEQS, p=P)

    def there(*js):
        return all(j.loop is not None or 0 <= j.at < rounds for j in js)

    def wait(eng, sem, value):
        if not isinstance(value, int) or value > 0:
            eng.wait_ge(sem, value)

    def run(eng, body, first, last, loop_first, loop_last):
        for i in range(first, loop_first):
            body(Round(i))
        pairs = (loop_last - loop_first + 1) // 2
        with eng.Fori(0, pairs) as it:
            body(Round(loop_first, it))
            body(Round(loop_first + 1, it))
        for i in range(loop_first + 2 * pairs, last + 1):
            body(Round(i))

    with ExitStack() as ctx:
        def sb(name, shape, dt=F32):
            return ctx.enter_context(nc.sbuf_tensor(name, shape, dt))

        def ps(name, shape):
            return ctx.enter_context(nc.psum_tensor(name, shape, F32))

        def sem(name):
            return ctx.enter_context(nc.semaphore(name))

        w_in = sb("w_in", [P, 4 * P])
        w_bc = sb("w_bc", [P, H, P])
        w_dt = sb("w_dt", [P, H * P])
        w_out = sb("w_out", [P, H, C])
        taps_w = sb("taps_w", [P, H, TAPS])
        conv_bias = sb("conv_bias", [P, H])
        dt_bias = sb("dt_bias", [P, H])
        skip_w = sb("skip_w", [P, H])
        a_neg = sb("a_neg", [P, H, NS])
        gate_w = sb("gate_w", [C, E])
        w1 = sb("w1", [C, E, FH, P])
        w2 = sb("w2", [P, FH, E, C])
        ident = sb("ident", [P, P])
        one_hot = sb("one_hot", [3 * SPLIT, 2 * NS], BF16)
        select = sb("select", [3 * SPLIT, 2 * NS, P], BF16)
        expert_no = sb("expert_no", [P, E])
        power = sb("power", [P, TB])
        quarter = sb("quarter", [P, TB])
        x_in = sb("x_in", [P, 2, TB, C])
        stats = sb("stats", [P, 2, TB, 6])
        moments = sb("moments", [P, 2, 4, TB])
        mean = sb("mean", [P, 2, TB])
        variance = sb("variance", [P, 2, TB])
        rstd = sb("rstd", [P, 2, TB])
        xn = sb("xn", [P, 2, TB, C])
        xnT = sb("xnT", [C, T])
        tap = sb("tap", [P, H, TAPS, SEQS, TAPS - 1 + SEQ])
        u = sb("u", [P, 2, H, T])
        gate = sb("gate", [P, 2, H, T])
        bcd = sb("bcd", [P, T])
        rest = sb("rest", [3 * SPLIT, T])
        mid = sb("mid", [3 * SPLIT, T], BF16)
        parts = sb("parts", [3 * SPLIT, 2, T], BF16)
        soft = sb("soft", [P, H, T])
        delta = sb("delta", [P, H, T])
        du = sb("du", [P, 2, H, T])
        dA = sb("dA", [P, 4, H, GROUP, T])
        h = sb("h", [P, RING, H, GROUP, T])
        c_rows = sb("c_rows", [P, 2, T])
        yT = sb("yT", [P, H, TB, P])
        yg = yT.rearrange("p h b t -> p h (b t)")
        x_again = sb("x_again", [P, 2, TB, C])
        x1 = sb("x1", [P, 2, TB, C])
        x2T = sb("x2T", [C, 2, T])
        scores = sb("scores", [P, TB, E])
        top = sb("top", [P, TB, 8])
        top_at = sb("top_at", [P, TB, 8], U32)
        top_no = sb("top_no", [P, TB, 2])
        ratio = sb("ratio", [P, TB])
        prob = sb("prob", [P, 3, TB])
        picked = sb("picked", [P, 2, TB, E])
        cw = sb("cw", [P, 2, TB, E])
        hid = sb("hid", [P, 2, FH, T])
        weighted = sb("weighted", [P, 2, TB, C])

        row_ps = [ps(f"row_ps{k}", [P, T]) for k in range(3)]
        y_ps = ps("y_ps", [P, H, TB, P])
        expert_ps = ps("expert_ps", [P, TB, C])
        bank = [ps("bank0", [P, T]), ps("bank1", [P, T])]

        weights_loaded = sem("weights_loaded")
        late_weights_loaded = sem("late_weights_loaded")
        one_hot_ready = sem("one_hot_ready")
        select_ready = sem("select_ready")
        zeros_set = sem("zeros_set")
        constants_ready = sem("constants_ready")
        a_exp_ready = sem("a_exp_ready")
        a_ready = sem("a_ready")
        x_loaded = [sem("x_loaded0"), sem("x_loaded1")]
        x_again_loaded = [sem("x_again_loaded0"), sem("x_again_loaded1")]
        out_stored = [sem("out_stored0"), sem("out_stored1")]
        stats_ready = [sem("stats_ready0"), sem("stats_ready1")]
        moments_ready = [sem("moments_ready0"), sem("moments_ready1")]
        variance_ready = [sem("variance_ready0"), sem("variance_ready1")]
        rstd_ready = [sem("rstd_ready0"), sem("rstd_ready1")]
        xn_ready = [sem("xn_ready0"), sem("xn_ready1")]
        xn_turned = sem("xn_turned")
        xnT_ready = sem("xnT_ready")
        projected = sem("projected")
        taps_ready = sem("taps_ready")
        gate_ready = sem("gate_ready")
        conv_added = sem("conv_added")
        u_ready = sem("u_ready")
        bcd_projected = sem("bcd_projected")
        bcd_ready = sem("bcd_ready")
        high_ready = sem("high_ready")
        split_step = sem("split_step")
        dt_projected = sem("dt_projected")
        dt_read = sem("dt_read")
        soft_exp = sem("soft_exp")
        soft_ready = sem("soft_ready")
        delta_ready = sem("delta_ready")
        du_ready = sem("du_ready")
        b_ready = sem("b_ready")
        c_ready = sem("c_ready")
        c_first_ready = sem("c_first_ready")
        dA_ready = sem("dA_ready")
        b_used = sem("b_used")
        scan_done = sem("scan_done")
        c_copied = sem("c_copied")
        c_first_used = sem("c_first_used")
        c_used = sem("c_used")
        y_added = sem("y_added")
        yT_ready = sem("yT_ready")
        y_turned = sem("y_turned")
        skip_added = sem("skip_added")
        gated = sem("gated")
        attn_projected = sem("attn_projected")
        x1_ready = sem("x1_ready")
        xn2_turned = sem("xn2_turned")
        x2T_ready = sem("x2T_ready")
        scored = sem("scored")
        scores_ready = sem("scores_ready")
        top_ready = sem("top_ready")
        top_gap = sem("top_gap")
        top_at_ready = sem("top_at_ready")
        ratio_ready = sem("ratio_ready")
        routing_step = sem("routing_step")
        hid_projected = sem("hid_projected")
        hid_ready = sem("hid_ready")
        expert_done = sem("expert_done")
        expert_weighted = sem("expert_weighted")
        expert_added = sem("expert_added")

        LOADS = 11
        LATE_LOADS = 4
        CONSTANTS = 7 + E
        block = ctx.enter_context(nc.Block())

        def spare(j, e):
            return j.loop is None and j.at >= rounds - 2 and e % 2

        def hidden_bank(j, e, f):
            return row_ps[f] if spare(j, e) else bank[f]

        def expert_bank(j, e):
            return row_ps[2].rearrange("p (b c) -> p b c", b=TB) if spare(j, e) else expert_ps

        @block.sync
        def _(sp):
            def load(dst, src):
                sp.dma_start(dst, src).then_inc(weights_loaded, 16)

            def load_late(dst, src):
                sp.dma_start(dst, src).then_inc(late_weights_loaded, 16)

            def start_round(i):
                nxt = i.later(3)
                if there(nxt):
                    wait(sp, xn_ready[0], nxt.count(1, -1))
                    sp.dma_start(x_in[:, nxt.odd], x_v[nxt.number()]).then_inc(x_loaded[nxt.odd], 16)
                if there(i):
                    wait(sp, x1_ready, i.count(1, -1))
                    sp.dma_start(x_again[:, i.odd], x_v[i.number()]).then_inc(x_again_loaded[i.odd], 16)
                done = i.later(-3)
                if there(done):
                    wait(sp, expert_added, done.count(E, E))
                    sp.dma_start(out_v[done.number()], x1[:, done.odd]).then_inc(out_stored[done.odd], 16)

            start_round(Round(-3))
            load(skip_w[:, :], D)
            load(w_in[:, :], W_in)
            start_round(Round(-2))
            load(taps_w[:, :, :], conv_w.rearrange("(h p) o k -> p h (o k)", p=P))
            load(conv_bias[:, :], conv_b)
            for part in range(3):
                load(w_bc[:, :, part * SPLIT:(part + 1) * SPLIT],
                     W_x[:, RANK:RANK + 2 * NS].rearrange("(h p) n -> p h n", p=P))
            load(w_bc[:, :, 3 * SPLIT:3 * SPLIT + RANK], W_x[:, 0:RANK].rearrange("(h p) n -> p h n", p=P))
            load(w_dt[3 * SPLIT:3 * SPLIT + RANK, :], W_dt)
            load(dt_bias[:, :], b_dt)
            load(a_neg[:, :, :], A_log.rearrange("(h p) n -> p h n", p=P))
            load_late(w_out[:, :, :], W_out.rearrange("(h p) c -> p h c", p=P))
            load_late(w1[:, :, :, :], w1T.rearrange("c (e h f) -> c e h f", e=E, h=FH))
            load_late(w2[:, :, :, :], w2T.rearrange("(h p) e c -> p h e c", p=P))
            load_late(gate_w[:, :], gate_wT)
            start_round(Round(-1))
            run(sp, start_round, 0, rounds + 2, 3, rounds - 4)
            for odd in range(2):
                sp.wait_ge(out_stored[odd], 16 * (rounds // 2))

        def convolve(eng, j, half):
            if not there(j):
                return
            total = tap[:, half, TAPS - 1, :, TAPS - 1:]
            for k in range(TAPS - 1):
                if k == 0:
                    eng.wait_ge(taps_ready, j.count(H, half + 1))
                else:
                    eng.wait_ge(conv_added, j.count(H * (TAPS - 1), half * (TAPS - 1) + k))
                eng.tensor_tensor(total, total, tap[:, half, k, :, k:k + SEQ],
                                  ALU.add).then_inc(conv_added, 1)

        def add_soft(eng, j):
            if not there(j):
                return
            eng.wait_ge(soft_ready, j.count(1, 1))
            eng.tensor_tensor(delta[:, :, :], delta[:, :, :], soft[:, :, :], ALU.add).then_inc(delta_ready, 1)

        def times_u(eng, j):
            if not there(j):
                return
            odd = j.odd
            eng.wait_ge(delta_ready, j.count(1, 1))
            eng.wait_ge(u_ready, j.count(H, H))
            wait(eng, b_used, j.count(CH * GROUP, -CH * GROUP))
            eng.tensor_tensor(du[:, odd], delta[:, :, :], u[:, odd], ALU.mult).then_inc(du_ready, 1)

        @block.gpsimd
        def _(pool):
            nc.gpsimd.memset(ident[:, :], 0.0).then_inc(zeros_set, 1)
            nc.gpsimd.memset(one_hot[:, :], 0.0).then_inc(zeros_set, 1)
            nc.gpsimd.memset(tap[:, :, 0:TAPS - 1, :, 0:TAPS - 1], 0.0).then_inc(constants_ready, 1)
            nc.gpsimd.memset(dA[:, :, :, :, 0:1], 0.0).then_inc(constants_ready, 1)
            nc.gpsimd.memset(dA[:, :, :, :, SEQ:SEQ + 1], 0.0).then_inc(constants_ready, 1)
            nc.gpsimd.memset(w_bc[:, :, 3 * SPLIT + RANK:], 0.0).then_inc(constants_ready, 1)
            nc.gpsimd.memset(power[:, :], -0.5).then_inc(constants_ready, 1)
            nc.gpsimd.memset(quarter[:, :], 0.25).then_inc(constants_ready, 1)
            for e in range(E):
                nc.gpsimd.memset(expert_no[:, e:e + 1], float(e)).then_inc(constants_ready, 1)
            pool.wait_ge(zeros_set, 2)
            nc.gpsimd.affine_select(out=ident[:, :], in_=ident[:, :], compare_op=ALU.not_equal, fill=1.0,
                                    base=0, pattern=[[-1, P]], channel_multiplier=1).then_inc(constants_ready, 1)
            pool.wait_ge(constants_ready, 7 + E)
            for part in range(3):
                nc.gpsimd.affine_select(out=one_hot[:, :], in_=one_hot[:, :], compare_op=ALU.not_equal,
                                        fill=1.0, base=-part * SPLIT, pattern=[[-1, 2 * NS]],
                                        channel_multiplier=1).then_inc(one_hot_ready, 1)
                pool.wait_ge(one_hot_ready, part + 1)

            def inverse_deviation(j, k):
                if not there(j):
                    return
                even, odd = ([stats[:, k, :, 3 * o + v] for v in (1, 2)] for o in range(2))
                total, gap, spread, square = (moments[:, k, v, :] for v in range(4))
                pool.wait_ge(stats_ready[k], j.count(1, 1))
                wait(pool, xn_ready[k], j.count(1, 0))
                nc.gpsimd.tensor_tensor(total, even[0], odd[0], ALU.add)
                nc.gpsimd.tensor_tensor(gap, even[0], odd[0], ALU.subtract)
                nc.gpsimd.tensor_tensor(spread, even[1], odd[1], ALU.add).then_inc(moments_ready[k], 1)
                pool.wait_ge(moments_ready[k], j.count(3, 1))
                nc.gpsimd.tensor_tensor(square, gap, quarter[:, :], ALU.mult)
                nc.gpsimd.tensor_scalar(mean[:, k, :], total, 0.5, None, ALU.mult)
                nc.gpsimd.tensor_scalar(spread, spread, 1.0 / C, EPS, ALU.mult, ALU.add).then_inc(moments_ready[k], 1)
                pool.wait_ge(moments_ready[k], j.count(3, 2))
                nc.gpsimd.tensor_tensor(square, square, gap, ALU.mult).then_inc(moments_ready[k], 1)
                pool.wait_ge(moments_ready[k], j.count(3, 3))
                nc.gpsimd.tensor_tensor(variance[:, k, :], spread, square, ALU.add).then_inc(variance_ready[k], 1)
                pool.wait_ge(variance_ready[k], j.count(1, 1))
                nc.gpsimd.tensor_tensor(rstd[:, k, :], variance[:, k, :], power[:, 0:TB],
                                        ALU.pow).then_inc(rstd_ready[k], 1)

            def split(j, *ran):
                if not there(j):
                    return
                odd = j.odd
                for s, k, per, more in ran:
                    if there(k):
                        wait(pool, s, k.count(per, more))
                pool.wait_ge(high_ready, j.count(1, 1))
                second, third = slice(SPLIT, 2 * SPLIT), slice(2 * SPLIT, 3 * SPLIT)
                nc.gpsimd.tensor_tensor(rest[third, :], bcd[third, :], parts[third, odd, :], ALU.subtract)
                nc.gpsimd.tensor_tensor(mid[third, :], bcd[third, :], parts[third, odd, :],
                                        ALU.subtract).then_inc(split_step, 1)
                pool.wait_ge(split_step, j.count(3, 1))
                nc.gpsimd.tensor_tensor(parts[second, odd, :], bcd[second, :], parts[second, odd, :],
                                        ALU.subtract).then_inc(split_step, 1)
                pool.wait_ge(split_step, j.count(3, 2))
                nc.gpsimd.tensor_tensor(parts[third, odd, :], rest[third, :], mid[third, :],
                                        ALU.subtract).then_inc(split_step, 1)
                pool.wait_ge(split_step, j.count(3, 3))

            def outputs(j, c):
                if not there(j):
                    return
                pool.wait_ge(c_copied, j.count(CH, c + 1))
                pool.wait_ge(scan_done, j.count(CH, c + 1))
                at = h[:, c % RING, :, 1, :]
                nc.gpsimd.tensor_tensor(at, at, c_rows[:, c % 2, :].unsqueeze(1).broadcast_to([P, H, T]),
                                        ALU.mult).then_inc(c_used, 1)

            def add_expert(j, e):
                if not there(j):
                    return
                pool.wait_ge(expert_weighted, j.count(E, e + 1))
                wait(pool, expert_added, j.count(E, e))
                nc.gpsimd.tensor_tensor(x1[:, j.odd], x1[:, j.odd], weighted[:, e % 2],
                                        ALU.add).then_inc(expert_added, 1)

            def round_(i):
                ahead, pre, post, moe, old = (i.later(k) for k in (2, 1, -1, -2, -3))
                convolve(pool, pre, 0)
                add_expert(old, 6)
                add_expert(old, 7)
                outputs(i, 0)
                outputs(i, 1)
                outputs(i, 2)
                convolve(pool, pre, 1)
                inverse_deviation(post, 1)
                add_expert(moe, 0)
                add_expert(moe, 1)
                outputs(i, 3)
                inverse_deviation(ahead, 0)
                add_expert(moe, 2)
                outputs(i, 4)
                split(pre,
                      (conv_added, pre, H * (TAPS - 1), 2 * (TAPS - 1)),
                      (c_used, i, CH, 5),
                      (expert_added, moe, E, 3),
                      (rstd_ready[1], post, 1, 1),
                      (rstd_ready[0], ahead, 1, 1),
                      (du_ready, i, 1, 1))
                outputs(i, 5)
                add_soft(pool, pre)
                add_expert(moe, 3)
                outputs(i, 6)
                times_u(pool, pre)
                add_expert(moe, 4)
                add_expert(moe, 5)
                outputs(i, 7)

            first, second, third = (Round(k) for k in range(3))
            inverse_deviation(first, 0)
            inverse_deviation(second, 0)
            split(first, (rstd_ready[0], second, 1, 1))
            convolve(pool, second, 0)
            outputs(first, 0)
            convolve(pool, second, 1)
            outputs(first, 1)
            inverse_deviation(third, 0)
            outputs(first, 2)
            outputs(first, 3)
            outputs(first, 4)
            split(second,
                  (c_used, first, CH, 5),
                  (rstd_ready[0], third, 1, 1),
                  (conv_added, second, H * (TAPS - 1), 2 * (TAPS - 1)))
            outputs(first, 5)
            add_soft(pool, second)
            times_u(pool, second)
            outputs(first, 6)
            outputs(first, 7)

            run(pool, round_, 1, rounds - 1, 3, rounds - 3)

            last_but_two, last_but_one, last = (Round(rounds - k) for k in (3, 2, 1))
            add_expert(last_but_two, 6)
            add_expert(last_but_two, 7)
            add_expert(last_but_one, 0)
            inverse_deviation(last, 1)
            add_expert(last_but_one, 1)
            add_expert(last_but_one, 2)
            add_expert(last_but_one, 3)
            add_expert(last_but_one, 4)
            add_expert(last_but_one, 5)
            add_expert(last_but_one, 6)
            add_expert(last_but_one, 7)
            add_expert(last, 0)
            add_expert(last, 1)
            add_expert(last, 2)
            add_expert(last, 3)
            add_expert(last, 4)
            add_expert(last, 5)
            add_expert(last, 6)
            add_expert(last, 7)

        @block.scalar
        def _(act):
            act.wait_ge(weights_loaded, 16 * LOADS)
            act.wait_ge(constants_ready, CONSTANTS)
            nc.scalar.activation(a_neg[:, :, :], a_neg[:, :, :], ACT.Exp).then_inc(a_exp_ready, 1)

            def decay(j, c):
                if not there(j):
                    return
                if c == 0:
                    act.wait_ge(delta_ready, j.count(1, 1))
                wait(act, scan_done, j.count(CH, c - 3))
                for half in range(H):
                    src = delta[:, half, :].rearrange("p (s t) -> p s t", s=SEQS)[:, :, 1:SEQ]
                    for n in range(GROUP):
                        dst = dA[:, c % 4, half, n, :].rearrange("p (s t) -> p s t", s=SEQS)[:, :, 1:SEQ]
                        k = c * GROUP + n
                        last = nc.scalar.activation(dst, src, ACT.Exp, scale=a_neg[:, half, k:k + 1])
                last.then_inc(dA_ready, 1)

            def copy_c(j, c):
                if not there(j):
                    return
                act.wait_ge(c_ready, j.count(CH, c + 1))
                wait(act, c_used, j.count(CH, c - 1))
                nc.scalar.activation(c_rows[:, c % 2, :], row_ps[2][:, :], ACT.Copy).then_inc(c_copied, 1)

            def copy_y(j):
                if not there(j):
                    return
                act.wait_ge(y_added, j.count(CH, CH))
                wait(act, attn_projected, j.count(1, 0))
                nc.scalar.activation(yT[:, :, :, :], y_ps[:, :, :, :], ACT.Copy).then_inc(yT_ready, 1)

            def hidden(j, e, f):
                if not there(j):
                    return
                wait(act, expert_done, j.count(E, e - 1))
                act.wait_ge(hid_projected, j.count(E * FH, FH * e + f + 1))
                nc.scalar.activation(hid[:, e % 2, f, :], hidden_bank(j, e, f)[:, :], ACT.Silu).then_inc(hid_ready, 1)

            def taps(j, half):
                if not there(j):
                    return
                wait(act, conv_added, j.count(H * (TAPS - 1), 0))
                wait(act, u_ready, j.count(H, 0))
                act.wait_ge(projected, j.count(2 * H, half + 1))
                for k in range(TAPS):
                    last = nc.scalar.activation(tap[:, half, k, :, TAPS - 1:],
                                                bank[half][:, :].rearrange("p (s t) -> p s t", s=SEQS),
                                                ACT.Copy, scale=taps_w[:, half, k:k + 1])
                last.then_inc(taps_ready, 1)

            def gate_silu(j, half):
                if not there(j):
                    return
                wait(act, gated, j.count(1, -1))
                act.wait_ge(projected, j.count(2 * H, H + half + 1))
                nc.scalar.activation(gate[:, j.odd, half, :], bank[half][:, :], ACT.Silu).then_inc(gate_ready, 1)

            def conv_silu(j, half):
                if not there(j):
                    return
                wait(act, gated, j.count(1, -1))
                act.wait_ge(conv_added, j.count(H * (TAPS - 1), (half + 1) * (TAPS - 1)))
                nc.scalar.activation(u[:, j.odd, half, :].rearrange("p (s t) -> p s t", s=SEQS),
                                     tap[:, half, TAPS - 1, :, TAPS - 1:], ACT.Silu,
                                     bias=conv_bias[:, half:half + 1]).then_inc(u_ready, 1)

            def copy_bcd(j):
                if not there(j):
                    return
                act.wait_ge(bcd_projected, j.count(1, 1))
                wait(act, split_step, j.count(3, 0))
                wait(act, dt_projected, j.count(H, 0))
                nc.scalar.activation(bcd[0:3 * SPLIT + RANK, :], bank[0][0:3 * SPLIT + RANK, :],
                                     ACT.Copy).then_inc(bcd_ready, 1)
                wait(act, c_first_ready, j.count(CH, -CH))
                nc.scalar.activation(parts[:, j.odd, :], bank[0][0:3 * SPLIT, :], ACT.Copy).then_inc(high_ready, 1)

            def soft_parts(j, half):
                if not there(j):
                    return
                wait(act, du_ready, j.count(1, 0))
                wait(act, dA_ready, j.count(CH, 0))
                act.wait_ge(dt_projected, j.count(H, half + 1))
                nc.scalar.activation(soft[:, half, :], bank[half][:, :], ACT.Abs,
                                     bias=dt_bias[:, half:half + 1])
                nc.scalar.activation(delta[:, half, :], bank[half][:, :], ACT.Relu,
                                     bias=dt_bias[:, half:half + 1]).then_inc(dt_read, 1)

            def soft_exponential(j):
                if not there(j):
                    return
                act.wait_ge(dt_read, j.count(H, H))
                nc.scalar.activation(soft[:, :, :], soft[:, :, :], ACT.Exp, scale=-1.0).then_inc(soft_exp, 1)

            def soft_log(j):
                if not there(j):
                    return
                act.wait_ge(soft_exp, j.count(1, 1))
                nc.scalar.activation(soft[:, :, :], soft[:, :, :], ACT.Ln, bias=1.0).then_inc(soft_ready, 1)

            def copy_x2T(j):
                if not there(j):
                    return
                act.wait_ge(xn2_turned, j.count(1, 1))
                wait(act, hid_projected, j.count(E * FH, -E * FH))
                nc.scalar.activation(x2T[:, j.odd, :], bank[1][:, :], ACT.Copy).then_inc(x2T_ready, 1)

            def copy_xnT(j):
                if not there(j):
                    return
                act.wait_ge(xn_turned, j.count(1, 1))
                wait(act, projected, j.count(2 * H, 0))
                nc.scalar.activation(xnT[:, :], bank[0][:, :], ACT.Copy).then_inc(xnT_ready, 1)

            def ratio_exp(j):
                if not there(j):
                    return
                act.wait_ge(top_gap, j.count(1, 1))
                nc.scalar.activation(ratio[:, :], ratio[:, :], ACT.Exp).then_inc(ratio_ready, 1)

            def round_(i):
                ahead, pre, post, moe = (i.later(k) for k in (2, 1, -1, -2))
                ratio_exp(moe)
                decay(i, 2)
                copy_c(i, 0)
                taps(pre, 1)
                hidden(moe, 0, 0)
                hidden(moe, 0, 1)
                copy_c(i, 1)
                copy_y(post)
                hidden(moe, 1, 0)
                hidden(moe, 1, 1)
                decay(i, 3)
                decay(i, 4)
                copy_c(i, 2)
                conv_silu(pre, 0)
                gate_silu(pre, 0)
                gate_silu(pre, 1)
                decay(i, 5)
                hidden(moe, 2, 0)
                copy_c(i, 3)
                hidden(moe, 2, 1)
                conv_silu(pre, 1)
                hidden(moe, 3, 0)
                hidden(moe, 3, 1)
                decay(i, 6)
                copy_bcd(pre)
                decay(i, 7)
                copy_c(i, 4)
                soft_parts(pre, 0)
                soft_parts(pre, 1)
                soft_exponential(pre)
                copy_x2T(post)
                hidden(moe, 4, 0)
                hidden(moe, 4, 1)
                copy_c(i, 5)
                hidden(moe, 5, 0)
                copy_xnT(ahead)
                hidden(moe, 5, 1)
                soft_log(pre)
                taps(ahead, 0)
                copy_c(i, 6)
                decay(pre, 0)
                hidden(moe, 6, 0)
                hidden(moe, 6, 1)
                copy_c(i, 7)
                hidden(moe, 7, 0)
                hidden(moe, 7, 1)
                decay(pre, 1)

            act.wait_ge(a_ready, 1)
            first, second, third = (Round(k) for k in range(3))
            copy_xnT(first)
            taps(first, 0)
            taps(first, 1)
            conv_silu(first, 0)
            gate_silu(first, 0)
            conv_silu(first, 1)
            copy_bcd(first)
            gate_silu(first, 1)
            soft_parts(first, 0)
            soft_parts(first, 1)
            soft_exponential(first)
            soft_log(first)
            copy_xnT(second)
            decay(first, 0)
            taps(second, 0)
            copy_c(first, 0)
            decay(first, 1)
            taps(second, 1)
            decay(first, 2)
            decay(first, 3)
            copy_c(first, 1)
            decay(first, 4)
            copy_c(first, 2)
            gate_silu(second, 0)
            conv_silu(second, 0)
            conv_silu(second, 1)
            copy_c(first, 3)
            gate_silu(second, 1)
            decay(first, 5)
            copy_c(first, 4)
            copy_bcd(second)
            decay(first, 6)
            decay(first, 7)
            copy_c(first, 5)
            soft_parts(second, 0)
            soft_parts(second, 1)
            soft_exponential(second)
            soft_log(second)
            copy_xnT(third)
            copy_c(first, 6)
            decay(second, 0)
            copy_c(first, 7)
            decay(second, 1)
            taps(third, 0)

            run(act, round_, 1, rounds - 1, 3, rounds - 3)

            last_but_two, last_but_one, last = (Round(rounds - k) for k in (3, 2, 1))
            ratio_exp(last_but_one)
            hidden(last_but_one, 0, 0)
            copy_y(last)
            hidden(last_but_one, 0, 1)
            hidden(last_but_one, 1, 0)
            hidden(last_but_one, 1, 1)
            hidden(last_but_one, 2, 0)
            hidden(last_but_one, 2, 1)
            hidden(last_but_one, 3, 0)
            hidden(last_but_one, 3, 1)
            copy_x2T(last)
            hidden(last_but_one, 4, 0)
            hidden(last_but_one, 4, 1)
            hidden(last_but_one, 5, 0)
            hidden(last_but_one, 5, 1)
            hidden(last_but_one, 6, 0)
            hidden(last_but_one, 6, 1)
            hidden(last_but_one, 7, 0)
            hidden(last_but_one, 7, 1)
            ratio_exp(last)
            hidden(last, 0, 0)
            hidden(last, 0, 1)
            hidden(last, 1, 0)
            hidden(last, 1, 1)
            hidden(last, 2, 0)
            hidden(last, 2, 1)
            hidden(last, 3, 0)
            hidden(last, 3, 1)
            hidden(last, 4, 0)
            hidden(last, 4, 1)
            hidden(last, 5, 0)
            hidden(last, 5, 1)
            hidden(last, 6, 0)
            hidden(last, 6, 1)
            hidden(last, 7, 0)
            hidden(last, 7, 1)

        @block.vector
        def _(dve):
            def inputs(j, c):
                if not there(j):
                    return
                if c == 0:
                    dve.wait_ge(du_ready, j.count(1, 1))
                wait(dve, y_added, j.count(CH, c + 1 - RING))
                for n in range(GROUP):
                    dve.wait_ge(b_ready, j.count(CH * GROUP, c * GROUP + n + 1))
                    nc.vector.tensor_tensor(h[:, c % RING, :, n, :], du[:, j.odd],
                                            row_ps[n][:, :].unsqueeze(1).broadcast_to([P, H, T]),
                                            ALU.mult).then_inc(b_used, 1)

            def scan(j, c):
                if not there(j):
                    return
                dve.wait_ge(b_used, j.count(CH * GROUP, c * GROUP + GROUP))
                dve.wait_ge(dA_ready, j.count(CH, c + 1))
                run_ = h[:, c % RING].rearrange("p h n t -> p (h n t)")
                nc.vector.tensor_tensor_scan(run_, dA[:, c % 4].rearrange("p h n t -> p (h n t)"), run_, 0.0,
                                             ALU.mult, ALU.add).then_inc(scan_done, 1)

            def outputs(j, c):
                if not there(j):
                    return
                dve.wait_ge(c_first_ready, j.count(CH, c + 1))
                dve.wait_ge(scan_done, j.count(CH, c + 1))
                at = h[:, c % RING, :, 0, :]
                nc.vector.tensor_tensor(at, at, row_ps[2][:, :].unsqueeze(1).broadcast_to([P, H, T]),
                                        ALU.mult).then_inc(c_first_used, 1)

            def norm_stats(j, k, src):
                wait(dve, variance_ready[k], j.count(1, 0))
                for b in range(TB):
                    last = nc.vector.bn_stats(stats[:, k, b, :], src[:, b, :])
                last.then_inc(stats_ready[k], 1)

            def norm_apply(j, k, src, turned):
                dve.wait_ge(rstd_ready[k], j.count(1, 1))
                wait(dve, turned, j.count(1, 0))
                for b in range(TB):
                    last = nc.vector.tensor_scalar(xn[:, k, b, :], src[:, b, :], mean[:, k, b:b + 1],
                                                   rstd[:, k, b:b + 1], ALU.subtract, ALU.mult)
                last.then_inc(xn_ready[k], 1)

            def pre_stats(j):
                if there(j):
                    dve.wait_ge(x_loaded[j.odd], j.turn(16, 16))
                    norm_stats(j, 0, x_in[:, j.odd])

            def pre_norm(j):
                if there(j):
                    norm_apply(j, 0, x_in[:, j.odd], xn_turned)

            def add_skip(j):
                if not there(j):
                    return
                dve.wait_ge(y_turned, j.count(H, H))
                for half in range(H):
                    nc.vector.scalar_tensor_tensor(out=yg[:, half, :], in0=u[:, j.odd, half, :],
                                                   scalar=skip_w[:, half:half + 1], in1=bank[half][:, :],
                                                   op0=ALU.mult, op1=ALU.add).then_inc(skip_added, 1)

            def gating(j):
                if not there(j):
                    return
                dve.wait_ge(skip_added, j.count(H, H))
                dve.wait_ge(gate_ready, j.count(H, H))
                nc.vector.tensor_tensor(yg[:, :, :], yg[:, :, :], gate[:, j.odd], ALU.mult).then_inc(gated, 1)

            def residual(j):
                if there(j):
                    dve.wait_ge(attn_projected, j.count(1, 1))
                    dve.wait_ge(x_again_loaded[j.odd], j.turn(16, 16))
                    wait(dve, out_stored[j.odd], j.turn(16, 0))
                    nc.vector.tensor_tensor(x1[:, j.odd], x_again[:, j.odd],
                                            bank[0][:, :].rearrange("p (b c) -> p b c", b=TB),
                                            ALU.add).then_inc(x1_ready, 1)

            def post_stats(j):
                if there(j):
                    dve.wait_ge(x1_ready, j.count(1, 1))
                    norm_stats(j, 1, x1[:, j.odd])

            def post_norm(j):
                if there(j):
                    norm_apply(j, 1, x1[:, j.odd], xn2_turned)

            def top_two(j):
                if not there(j):
                    return
                dve.wait_ge(scored, j.count(1, 1))
                in_bank = bank[1][:, 0:TB * E].rearrange("p (b e) -> p b e", b=TB)
                nc.vector.tensor_copy(scores[:, :, :], in_bank).then_inc(scores_ready, 1)
                for b in range(TB):
                    last = nc.vector.max(out=top[:, b, :], in_=in_bank[:, b, :])
                last.then_inc(top_ready, 1)
                dve.wait_ge(scores_ready, j.count(1, 1))
                dve.wait_ge(top_ready, j.count(1, 1))
                nc.vector.tensor_tensor(ratio[:, :], top[:, :, 1], top[:, :, 0], ALU.subtract).then_inc(top_gap, 1)
                for b in range(TB):
                    last = nc.vector.max_index(top_at[:, b, :], top[:, b, :], scores[:, b, :])
                last.then_inc(top_at_ready, 1)

            def routing(j):
                if not there(j):
                    return
                step = 0

                def then(ins):
                    nonlocal step
                    step += 1
                    ins.then_inc(routing_step, 1)

                def so_far():
                    dve.wait_ge(routing_step, j.count(8, step))

                dve.wait_ge(ratio_ready, j.count(1, 1))
                dve.wait_ge(top_at_ready, j.count(1, 1))
                then(nc.vector.tensor_scalar(prob[:, 0, :], ratio[:, :], 1.0, None, ALU.add))
                then(nc.vector.tensor_copy(top_no[:, :, :], top_at[:, :, 0:2]))
                so_far()
                then(nc.vector.reciprocal(prob[:, 1, :], prob[:, 0, :]))
                for k in range(2):
                    no = top_no[:, :, k:k + 1].broadcast_to([P, TB, E])
                    then(nc.vector.tensor_tensor(picked[:, k], expert_no[:, :].unsqueeze(1).broadcast_to([P, TB, E]),
                                                 no, ALU.is_equal))
                so_far()
                nc.vector.tensor_tensor(prob[:, 2, :], ratio[:, :], prob[:, 1, :], ALU.mult).then_inc(routing_step, 1)
                step += 1
                so_far()
                for k in range(2):
                    pk = prob[:, 1 + k, :].unsqueeze(2).broadcast_to([P, TB, E])
                    last = nc.vector.tensor_tensor(picked[:, k], picked[:, k], pk, ALU.mult)
                then(last)
                so_far()
                then(nc.vector.tensor_tensor(cw[:, j.odd], picked[:, 0], picked[:, 1], ALU.add))

            def weight_expert(j, e):
                if not there(j):
                    return
                dve.wait_ge(expert_done, j.count(E, e + 1))
                if e == 0:
                    dve.wait_ge(routing_step, j.count(8, 8))
                wait(dve, expert_added, j.count(E, e - 1))
                nc.vector.tensor_tensor(weighted[:, e % 2], expert_bank(j, e)[:, :, :],
                                        cw[:, j.odd, :, e:e + 1].broadcast_to([P, TB, C]),
                                        ALU.mult).then_inc(expert_weighted, 1)

            def round_(i):
                ahead, post, moe, old = i.later(2), i.later(-1), i.later(-2), i.later(-3)
                inputs(i, 0)
                outputs(post, 7)
                weight_expert(old, 6)
                scan(i, 0)
                inputs(i, 1)
                weight_expert(old, 7)
                outputs(i, 0)
                scan(i, 1)
                inputs(i, 2)
                outputs(i, 1)
                add_skip(post)
                routing(moe)
                gating(post)
                scan(i, 2)
                weight_expert(moe, 0)
                inputs(i, 3)
                residual(post)
                outputs(i, 2)
                weight_expert(moe, 1)
                post_stats(post)
                scan(i, 3)
                inputs(i, 4)
                post_norm(post)
                weight_expert(moe, 2)
                pre_stats(ahead)
                outputs(i, 3)
                scan(i, 4)
                pre_norm(ahead)
                outputs(i, 4)
                inputs(i, 5)
                weight_expert(moe, 3)
                scan(i, 5)
                inputs(i, 6)
                weight_expert(moe, 4)
                outputs(i, 5)
                scan(i, 6)
                top_two(post)
                inputs(i, 7)
                outputs(i, 6)
                weight_expert(moe, 5)
                scan(i, 7)

            first, second, third = (Round(k) for k in range(3))
            pre_stats(first)
            dve.wait_ge(one_hot_ready, 3)
            nc.vector.tensor_copy(select[:, :, :], one_hot[:, :].unsqueeze(2).broadcast_to([3 * SPLIT, 2 * NS, P])
                                  ).then_inc(select_ready, 1)
            dve.wait_ge(constants_ready, CONSTANTS)
            dve.wait_ge(weights_loaded, 16 * LOADS)
            dve.wait_ge(a_exp_ready, 1)
            nc.vector.tensor_scalar(a_neg[:, :, :], a_neg[:, :, :], -1.0, None, ALU.mult).then_inc(a_ready, 1)
            pre_stats(second)
            pre_norm(first)
            pre_norm(second)
            pre_stats(third)
            convolve(dve, first, 0)
            convolve(dve, first, 1)
            add_soft(dve, first)
            times_u(dve, first)
            inputs(first, 0)
            inputs(first, 1)
            scan(first, 0)
            inputs(first, 2)
            scan(first, 1)
            outputs(first, 0)
            scan(first, 2)
            inputs(first, 3)
            outputs(first, 1)
            scan(first, 3)
            outputs(first, 2)
            inputs(first, 4)
            outputs(first, 3)
            inputs(first, 5)
            scan(first, 4)
            pre_norm(third)
            outputs(first, 4)
            scan(first, 5)
            inputs(first, 6)
            outputs(first, 5)
            scan(first, 6)
            inputs(first, 7)
            outputs(first, 6)
            scan(first, 7)

            run(dve, round_, 1, rounds - 1, 3, rounds - 3)

            last_but_two, last_but_one, last = (Round(rounds - k) for k in (3, 2, 1))
            outputs(last, 7)
            weight_expert(last_but_two, 6)
            routing(last_but_one)
            weight_expert(last_but_two, 7)
            add_skip(last)
            gating(last)
            weight_expert(last_but_one, 0)
            residual(last)
            post_stats(last)
            weight_expert(last_but_one, 1)
            post_norm(last)
            top_two(last)
            weight_expert(last_but_one, 2)
            weight_expert(last_but_one, 3)
            weight_expert(last_but_one, 4)
            weight_expert(last_but_one, 5)
            weight_expert(last_but_one, 6)
            weight_expert(last_but_one, 7)
            routing(last)
            weight_expert(last, 0)
            weight_expert(last, 1)
            weight_expert(last, 2)
            weight_expert(last, 3)
            weight_expert(last, 4)
            weight_expert(last, 5)
            weight_expert(last, 6)
            weight_expert(last, 7)

        @block.tensor
        def _(pe):
            def free(*uses):
                for s, j, per, more in uses:
                    if there(j):
                        pe.wait_ge(s, j.count(per, more))
                        return

            def broadcast(dst, j, row, ready):
                nc.tensor.matmul(dst[:, :], select[:, row, :], parts[:, j.odd, :], start=True,
                                 stop=True).then_inc(ready, 1)

            def rows_b(j, c):
                if not there(j):
                    return
                if c == 0:
                    pe.wait_ge(split_step, j.count(3, 3))
                for n in range(GROUP):
                    wait(pe, b_used, j.count(CH * GROUP, (c - 1) * GROUP + n + 1))
                    broadcast(row_ps[n], j, c * GROUP + n, b_ready)

            def row_c(j, c):
                if not there(j):
                    return
                if c == 0:
                    pe.wait_ge(split_step, j.count(3, 3))
                wait(pe, c_first_used, j.count(CH, c))
                broadcast(row_ps[2], j, NS + c * GROUP + 1, c_ready)

            def row_c_first(j, c):
                if not there(j):
                    return
                pe.wait_ge(c_copied, j.count(CH, c + 1))
                broadcast(row_ps[2], j, NS + c * GROUP, c_first_ready)

            def sum_states(j, c):
                if not there(j):
                    return
                pe.wait_ge(c_first_used, j.count(CH, c + 1))
                pe.wait_ge(c_used, j.count(CH, c + 1))
                if c == 0:
                    wait(pe, yT_ready, j.count(1, 0))
                for half in range(H):
                    for n in range(GROUP):
                        for b in range(TB):
                            last = nc.tensor.matmul(y_ps[:, half, b, :], h[:, c % RING, half, n, b * P:(b + 1) * P],
                                                    ident[:, :], is_transpose=True,
                                                    start=(c == 0 and n == 0 and b == 0),
                                                    stop=(c == CH - 1 and n == GROUP - 1), skip_group_check=True)
                last.then_inc(y_added, 1)

            def turn(dst, src, signal):
                for b in range(TB):
                    last = nc.tensor.transpose(dst[:, b * P:(b + 1) * P], src[:, b, :], ident[:, :])
                last.then_inc(signal, 1)

            def hidden(j, e, f, *uses):
                if not there(j):
                    return
                if e == 0 and f == 0:
                    pe.wait_ge(x2T_ready, j.count(1, 1))
                free(*uses)
                nc.tensor.matmul(hidden_bank(j, e, f)[:, :], w1[:, e, f, :], x2T[:, j.odd, :], start=True,
                                 stop=True).then_inc(hid_projected, 1)

            def expert(j, e):
                if not there(j):
                    return
                pe.wait_ge(hid_ready, j.count(E * FH, FH * (e + 1)))
                if spare(j, 1) and (j.at, e) == (rounds - 2, 1):
                    pe.wait_ge(c_first_used, rounds * CH)
                elif spare(j, 1) and (j.at, e) != (rounds - 2, 0):
                    pe.wait_ge(expert_weighted, j.count(E, e - 1))
                else:
                    wait(pe, expert_weighted, j.count(E, e))
                for b in range(TB):
                    for f in range(FH):
                        last = nc.tensor.matmul(expert_bank(j, e)[:, b, :], hid[:, e % 2, f, b * P:(b + 1) * P],
                                                w2[:, f, e, :], start=(f == 0), stop=(f == FH - 1))
                last.then_inc(expert_done, 1)

            def project(j, f, *uses):
                if not there(j):
                    return
                if f == 0:
                    pe.wait_ge(xnT_ready, j.count(1, 1))
                free(*uses)
                nc.tensor.matmul(bank[f % H][:, :], w_in[:, f * P:(f + 1) * P], xnT[:, :], start=True,
                                 stop=True).then_inc(projected, 1)

            def turn_y(j, half, *uses):
                if not there(j):
                    return
                pe.wait_ge(yT_ready, j.count(1, 1))
                free(*uses)
                turn(bank[half], yT[:, half], y_turned)

            def turn_x(j, *uses):
                if not there(j):
                    return
                pe.wait_ge(xn_ready[0], j.count(1, 1))
                free(*uses)
                turn(bank[0], xn[:, 0], xn_turned)

            def turn_x2(j, *uses):
                if not there(j):
                    return
                pe.wait_ge(xn_ready[1], j.count(1, 1))
                free(*uses)
                turn(bank[1], xn[:, 1], xn2_turned)

            def project_out(j, *uses):
                if not there(j):
                    return
                if j.loop is None and j.at == 0:
                    pe.wait_ge(late_weights_loaded, 16 * LATE_LOADS)
                pe.wait_ge(gated, j.count(1, 1))
                free(*uses)
                for b in range(TB):
                    for half in range(H):
                        last = nc.tensor.matmul(bank[0][:, b * C:(b + 1) * C], yg[:, half, b * P:(b + 1) * P],
                                                w_out[:, half, :], start=(half == 0), stop=(half == H - 1))
                last.then_inc(attn_projected, 1)

            def project_bcd(j, *uses):
                if not there(j):
                    return
                pe.wait_ge(u_ready, j.count(H, H))
                free(*uses)
                for half in range(H):
                    last = nc.tensor.matmul(bank[0][:, :], w_bc[:, half, :], u[:, j.odd, half, :],
                                            start=(half == 0), stop=(half == H - 1))
                last.then_inc(bcd_projected, 1)

            def delta_rank(j, half, *uses):
                if not there(j):
                    return
                pe.wait_ge(bcd_ready, j.count(1, 1))
                free(*uses)
                rows = slice(3 * SPLIT, 3 * SPLIT + RANK)
                nc.tensor.matmul(bank[half][:, :], w_dt[rows, half * P:(half + 1) * P], bcd[rows, :],
                                 start=True, stop=True).then_inc(dt_projected, 1)

            def score(j, *uses):
                if not there(j):
                    return
                pe.wait_ge(x2T_ready, j.count(1, 1))
                free(*uses)
                for b in range(TB):
                    last = nc.tensor.matmul(bank[1][:, b * E:(b + 1) * E], x2T[:, j.odd, b * P:(b + 1) * P],
                                            gate_w[:, :], start=True, stop=True)
                last.then_inc(scored, 1)

            def use_hid(j, e, f):
                return (hid_ready, j, E * FH, FH * e + f + 1)

            def use_xi(j, half):
                return (taps_ready, j, H, half + 1)

            def use_gate(j, half):
                return (gate_ready, j, H, half + 1)

            def use_y(j, half):
                return (skip_added, j, H, half + 1)

            def use_attn(j):
                return (x1_ready, j, 1, 1)

            def use_bcd(j):
                return (high_ready, j, 1, 1)

            def use_dt(j, half):
                return (dt_read, j, H, half + 1)

            def use_x2T(j):
                return (x2T_ready, j, 1, 1)

            def use_scores(j):
                return (top_ready, j, 1, 1)

            def use_xnT(j):
                return (xnT_ready, j, 1, 1)

            def round_(i):
                ahead, pre, post, moe, old = (i.later(k) for k in (2, 1, -1, -2, -3))
                project(pre, 1, use_hid(old, 7, 1), use_scores(moe), use_dt(i, 1))
                expert(old, 6)
                row_c(i, 0)
                rows_b(i, 1)
                expert(old, 7)
                row_c_first(i, 0)
                hidden(moe, 0, 0, use_hid(old, 7, 0), use_xi(pre, 0), use_dt(i, 0), use_attn(moe))
                sum_states(post, 7)
                hidden(moe, 0, 1, use_xi(pre, 1), use_hid(old, 7, 1), use_scores(moe))
                rows_b(i, 2)
                row_c(i, 1)
                hidden(moe, 1, 0, use_hid(moe, 0, 0))
                hidden(moe, 1, 1, use_hid(moe, 0, 1))
                row_c_first(i, 1)
                turn_y(post, 0, use_hid(moe, 1, 0), use_xi(pre, 0), use_dt(i, 0))
                turn_y(post, 1, use_hid(moe, 1, 1), use_xi(pre, 1), use_dt(i, 1))
                sum_states(i, 0)
                row_c(i, 2)
                sum_states(i, 1)
                project(pre, 2, use_y(post, 0), use_xi(pre, 0))
                project(pre, 3, use_y(post, 1), use_xi(pre, 1))
                rows_b(i, 3)
                expert(moe, 0)
                row_c_first(i, 2)
                project_out(post, use_gate(pre, 0), use_y(post, 0))
                expert(moe, 1)
                hidden(moe, 2, 0, use_attn(post), use_hid(moe, 1, 0))
                hidden(moe, 2, 1, use_gate(pre, 1), use_y(post, 1), use_hid(moe, 1, 1))
                row_c(i, 3)
                rows_b(i, 4)
                hidden(moe, 3, 0, use_hid(moe, 2, 0))
                row_c_first(i, 3)
                hidden(moe, 3, 1, use_hid(moe, 2, 1))
                expert(moe, 2)
                project_bcd(pre, use_hid(moe, 3, 0), use_attn(post), use_gate(pre, 0))
                sum_states(i, 2)
                expert(moe, 3)
                row_c(i, 4)
                delta_rank(pre, 0, use_bcd(pre))
                delta_rank(pre, 1, use_hid(moe, 3, 1), use_gate(pre, 1))
                row_c_first(i, 4)
                rows_b(i, 5)
                sum_states(i, 3)
                turn_x2(post, use_dt(pre, 1), use_hid(moe, 3, 1), use_y(post, 1))
                row_c(i, 5)
                hidden(moe, 4, 0, use_dt(pre, 0), use_hid(moe, 3, 0))
                rows_b(i, 6)
                hidden(moe, 4, 1, use_x2T(post), use_hid(moe, 3, 1))
                hidden(moe, 5, 0, use_hid(moe, 4, 0))
                hidden(moe, 5, 1, use_hid(moe, 4, 1))
                turn_x(ahead, use_hid(moe, 5, 0), use_dt(pre, 0))
                expert(moe, 4)
                project(ahead, 0, use_xnT(ahead))
                row_c_first(i, 5)
                sum_states(i, 4)
                row_c(i, 6)
                score(post, use_hid(moe, 5, 1), use_x2T(post))
                rows_b(i, 7)
                hidden(moe, 6, 0, use_xi(ahead, 0), use_hid(moe, 5, 0))
                sum_states(i, 5)
                row_c_first(i, 6)
                expert(moe, 5)
                hidden(moe, 6, 1, use_scores(post), use_hid(moe, 5, 1))
                rows_b(pre, 0)
                row_c(i, 7)
                hidden(moe, 7, 0, use_hid(moe, 6, 0))
                hidden(moe, 7, 1, use_hid(moe, 6, 1))
                row_c_first(i, 7)
                sum_states(i, 6)

            pe.wait_ge(constants_ready, CONSTANTS)
            pe.wait_ge(weights_loaded, 16 * LOADS)
            pe.wait_ge(select_ready, 1)
            first, second, third = (Round(k) for k in range(3))
            turn_x(first)
            project(first, 0, use_xnT(first))
            project(first, 1)
            project(first, 2, use_xi(first, 0))
            project_bcd(first, use_gate(first, 0))
            project(first, 3, use_xi(first, 1))
            delta_rank(first, 0, use_bcd(first))
            delta_rank(first, 1, use_gate(first, 1))
            turn_x(second, use_dt(first, 0))
            project(second, 0, use_xnT(second))
            rows_b(first, 0)
            row_c(first, 0)
            project(second, 1, use_dt(first, 1))
            rows_b(first, 1)
            rows_b(first, 2)
            row_c_first(first, 0)
            project(second, 2, use_xi(second, 0))
            row_c(first, 1)
            rows_b(first, 3)
            row_c_first(first, 1)
            project(second, 3, use_xi(second, 1))
            sum_states(first, 0)
            rows_b(first, 4)
            row_c(first, 2)
            row_c_first(first, 2)
            sum_states(first, 1)
            row_c(first, 3)
            row_c_first(first, 3)
            rows_b(first, 5)
            row_c(first, 4)
            project_bcd(second, use_gate(second, 0))
            sum_states(first, 2)
            row_c_first(first, 4)
            delta_rank(second, 0, use_bcd(second))
            rows_b(first, 6)
            row_c(first, 5)
            delta_rank(second, 1, use_gate(second, 1))
            row_c_first(first, 5)
            sum_states(first, 3)
            rows_b(first, 7)
            sum_states(first, 4)
            row_c(first, 6)
            turn_x(third, use_dt(second, 0))
            row_c_first(first, 6)
            rows_b(second, 0)
            row_c(first, 7)
            sum_states(first, 5)
            row_c_first(first, 7)
            project(third, 0, use_xnT(third))
            sum_states(first, 6)

            run(pe, round_, 1, rounds - 1, 3, rounds - 3)

            last_but_two, last_but_one, last = (Round(rounds - k) for k in (3, 2, 1))
            hidden(last_but_one, 0, 0, use_hid(last_but_two, 7, 0))
            hidden(last_but_one, 0, 1, use_hid(last_but_two, 7, 1))
            expert(last_but_two, 6)
            sum_states(last, 7)
            hidden(last_but_one, 1, 0, (b_used, last, CH * GROUP, CH * GROUP))
            expert(last_but_two, 7)
            turn_y(last, 0, use_hid(last_but_one, 0, 0))
            turn_y(last, 1, use_hid(last_but_one, 0, 1))
            expert(last_but_one, 0)
            hidden(last_but_one, 1, 1, (b_used, last, CH * GROUP, CH * GROUP))
            hidden(last_but_one, 2, 0, use_y(last, 0))
            hidden(last_but_one, 2, 1, use_y(last, 1))
            project_out(last, use_hid(last_but_one, 2, 0))
            hidden(last_but_one, 3, 0, use_hid(last_but_one, 1, 0))
            hidden(last_but_one, 3, 1, use_hid(last_but_one, 1, 1))
            expert(last_but_one, 1)
            expert(last_but_one, 2)
            expert(last_but_one, 3)
            turn_x2(last, use_hid(last_but_one, 2, 1))
            hidden(last_but_one, 4, 0, use_attn(last))
            hidden(last_but_one, 4, 1, use_x2T(last))
            hidden(last_but_one, 5, 0, use_hid(last_but_one, 3, 0))
            score(last, use_hid(last_but_one, 4, 1))
            hidden(last_but_one, 5, 1, use_hid(last_but_one, 3, 1))
            hidden(last_but_one, 6, 0, use_hid(last_but_one, 4, 0))
            hidden(last_but_one, 6, 1, use_scores(last))
            expert(last_but_one, 4)
            hidden(last_but_one, 7, 0, use_hid(last_but_one, 5, 0))
            expert(last_but_one, 5)
            hidden(last_but_one, 7, 1, use_hid(last_but_one, 5, 1))
            hidden(last, 0, 0, use_hid(last_but_one, 6, 0))
            hidden(last, 0, 1, use_hid(last_but_one, 6, 1))
            expert(last_but_one, 6)
            expert(last_but_one, 7)
            hidden(last, 1, 0, use_hid(last_but_one, 7, 0))
            expert(last, 0)
            hidden(last, 1, 1, use_hid(last_but_one, 7, 1))
            hidden(last, 2, 0, use_hid(last, 0, 0))
            expert(last, 1)
            hidden(last, 2, 1, use_hid(last, 0, 1))
            hidden(last, 3, 0, use_hid(last, 1, 0))
            hidden(last, 3, 1, use_hid(last, 1, 1))
            hidden(last, 4, 0, use_hid(last, 2, 0))
            expert(last, 2)
            expert(last, 3)
            hidden(last, 4, 1, use_hid(last, 2, 1))
            hidden(last, 5, 0, use_hid(last, 3, 0))
            hidden(last, 5, 1, use_hid(last, 3, 1))
            hidden(last, 6, 0, use_hid(last, 4, 0))
            hidden(last, 6, 1, use_hid(last, 4, 1))
            expert(last, 4)
            expert(last, 5)
            hidden(last, 7, 0, use_hid(last, 5, 0))
            hidden(last, 7, 1, use_hid(last, 5, 1))
            expert(last, 6)
            expert(last, 7)


_INS = ['x', 'W_in', 'conv_w', 'conv_b', 'W_x', 'W_dt', 'b_dt', 'A_log', 'D', 'W_out']


def kernel(**inputs):
    import numpy as _np
    import concourse.bacc as _bacc
    from concourse import mybir as _mybir
    from concourse.bass_utils import run_bass_kernel_spmd as _run

    host = {name: inputs[f"L0_attn_{name}"] for name in _INS}
    for name in ("conv_b", "b_dt", "D"):
        host[name] = _np.asarray(host[name]).reshape(H, P).T
    w1, w2 = _np.asarray(inputs["L0_ffn_w1"]), _np.asarray(inputs["L0_ffn_w2"])
    host["gate_wT"] = _np.asarray(inputs["L0_ffn_gate_w"]).T
    host["w1T"] = w1.reshape(-1, w1.shape[2]).T
    host["w2T"] = w2.transpose(2, 0, 1)

    nc = _bacc.Bacc("TRN2", target_bir_lowering=False, num_devices=1)
    arrays, args = {}, []
    for name, a in host.items():
        a = _np.ascontiguousarray(a)
        arrays[f"in_{name}"] = a
        args.append(nc.dram_tensor(f"in_{name}", a.shape, _mybir.dt.from_np(a.dtype), kind="ExternalInput").ap())
    shape = tuple(host["x"].shape)
    args.append(nc.dram_tensor("out_0", shape, _mybir.dt.float32, kind="ExternalOutput").ap())
    mamba_moe(nc, *args)
    r = _run(nc, [arrays], core_ids=[0])
    return r.results[0]["out_0"]
```
